# Optimizing a Trainium2 kernel written in Bass

```python
import numpy as np
import jax
import jax.numpy as jnp

def _softmax(x, axis=-1):
    return jax.nn.softmax(x, axis=axis)

def _gelu(x):
    return jax.nn.gelu(x, approximate=True)

def _silu(x):
    return jax.nn.silu(x)

def _sigmoid(x):
    return jax.nn.sigmoid(x)

def _layernorm(x, axis=-1, eps=1e-05):
    m = jnp.mean(x, axis=axis, keepdims=True)
    v = jnp.var(x, axis=axis, keepdims=True)
    return (x - m) / jnp.sqrt(v + eps)

def _scatter_add(tgt, idx, src, axis=0):
    return tgt.at[idx].add(src)

def _segment_sum(src, seg, n):
    return jax.ops.segment_sum(src, seg, n)
kernel_name = 'mk_cond_resid_d2_seqx_r4_e4ed41'

def setup_inputs(seed: int=0):
    np.random.seed(seed)
    _w = jnp.asarray

    def _rec_inputs():
        import jax
        import jax.numpy as jnp
        _rk = jax.random.key(seed)
        x = -5.13e-06 + 0.01765 * jax.random.normal(jax.random.fold_in(_rk, 1), (2, 1024, 256), jnp.float32)
        _lenS = 1024 - jax.random.randint(jax.random.fold_in(_rk, 7), (2,), 0, max(1, 1024 // 4) + 1, jnp.int32)
        _lenS2 = 1024 - jax.random.randint(jax.random.fold_in(_rk, 8), (2,), 0, max(1, 1024 // 4) + 1, jnp.int32)
        cond_1024 = 0.0061147 + 1.02565 * jax.random.normal(jax.random.fold_in(_rk, 11), (2, 256), jnp.float32)
        return (x, cond_1024)
    x, cond_1024 = _rec_inputs()

    def _L0_cond_setup():
        import math
        import jax, jax.numpy as jnp
        import numpy as np
        EPS = 1e-07
        MAX_TANH_ARG = 1.0 - 1e-05

        def _norm(x):
            return jnp.sqrt(jnp.sum(x * x, axis=-1, keepdims=True)).clip(EPS)

        def logmap0(x):
            n = _norm(x)
            return jnp.arctanh(jnp.clip(n, EPS, MAX_TANH_ARG)) * x / n

        def expmap0(v):
            n = _norm(v)
            return jnp.tanh(n) * v / n

        def mobius_add(x, y):
            x2 = jnp.sum(x * x, -1, keepdims=True)
            y2 = jnp.sum(y * y, -1, keepdims=True)
            xy = jnp.sum(x * y, -1, keepdims=True)
            num = (1 + 2 * xy + y2) * x + (1 - x2) * y
            den = (1 + 2 * xy + x2 * y2).clip(EPS)
            return num / den

        def plin(x, w, b):
            return expmap0(logmap0(x) @ w + b)

        def layer_norm(x, eps=1e-06):
            m = x.mean(-1, keepdims=True)
            v = ((x - m) ** 2).mean(-1, keepdims=True)
            return (x - m) / jnp.sqrt(v + eps)

        def _beta(a, b):
            return math.exp(math.lgamma(a) + math.lgamma(b) - math.lgamma(a + b))
        D, H, FF = (256, 16, 1024)
        HD = D // H
        BETA_N = _beta(D / 2, 0.5)
        BETA_H = _beta(HD / 2, 0.5)

        def _to_heads(p):
            B, S, _ = p.shape
            t = logmap0(p).reshape(B, S, H, HD) * (BETA_H / BETA_N)
            return expmap0(jnp.transpose(t, (0, 2, 1, 3)))

        def _from_heads(ph):
            B, _, S, _ = ph.shape
            t = logmap0(ph) * (BETA_N / BETA_H)
            t = jnp.transpose(t, (0, 2, 1, 3)).reshape(B, S, D)
            return expmap0(t)
        key = jax.random.key(seed)
        ks = jax.random.split(key, 20)
        B, S = (4, 256)
        x = expmap0(0.02 * jax.random.normal(ks[0], (B, S, D), jnp.float32))
        t_emb = jax.random.normal(ks[1], (B, 1, D), jnp.float32)
        g = lambda k, sh: 0.02 * jax.random.normal(k, sh, jnp.float32)
        return {'x': x, 't_emb': t_emb, 'w_q': g(ks[2], (D, D)), 'b_q': jnp.zeros((D,), jnp.float32), 'w_k': g(ks[3], (D, D)), 'b_k': jnp.zeros((D,), jnp.float32), 'w_v': g(ks[4], (D, D)), 'b_v': jnp.zeros((D,), jnp.float32), 'w_o': g(ks[5], (D, D)), 'b_o': jnp.zeros((D,), jnp.float32), 'w_f1': g(ks[6], (D, FF)), 'b_f1': jnp.zeros((FF,), jnp.float32), 'w_f2': g(ks[7], (FF, D)), 'b_f2': jnp.zeros((D,), jnp.float32), 'w_ada': g(ks[8], (D, 6 * D)), 'b_ada': jnp.zeros((6 * D,), jnp.float32)}
    _L0_cond_all = _L0_cond_setup()
    _L0_cond_in = {k: v for k, v in _L0_cond_all.items() if k in ('w_q', 'b_q', 'w_k', 'b_k', 'w_v', 'b_v', 'w_o', 'b_o', 'w_f1', 'b_f1', 'w_f2', 'b_f2', 'w_ada', 'b_ada')}
    del _L0_cond_all

    def _L1_cond_setup():
        import jax, jax.numpy as jnp
        import numpy as np
        N, T, D, H = (64, 64, 256, 256)
        key = jax.random.key(seed)
        k1, k2, k3, k4 = jax.random.split(key, 4)
        x = jax.random.normal(k1, (N, T, D), dtype=jnp.float32)
        h0 = jax.random.normal(k2, (N, H), dtype=jnp.float32)
        Wx = jax.random.normal(k3, (D, H), dtype=jnp.float32) / jnp.sqrt(jnp.float32(D))
        Wh = jax.random.normal(k4, (H, H), dtype=jnp.float32) / jnp.sqrt(jnp.float32(H))
        b = jnp.zeros((H,), dtype=jnp.float32)
        return {'x': x, 'h0': h0, 'Wx': Wx, 'Wh': Wh, 'b': b}
    _L1_cond_all = _L1_cond_setup()
    _L1_cond_in = {k: v for k, v in _L1_cond_all.items() if k in ('Wx', 'Wh', 'b')}
    del _L1_cond_all
    return {'x': x, 'cond_1024': cond_1024, 'L0_cond_w_q': _L0_cond_in['w_q'], 'L0_cond_b_q': _L0_cond_in['b_q'], 'L0_cond_w_k': _L0_cond_in['w_k'], 'L0_cond_b_k': _L0_cond_in['b_k'], 'L0_cond_w_v': _L0_cond_in['w_v'], 'L0_cond_b_v': _L0_cond_in['b_v'], 'L0_cond_w_o': _L0_cond_in['w_o'], 'L0_cond_b_o': _L0_cond_in['b_o'], 'L0_cond_w_f1': _L0_cond_in['w_f1'], 'L0_cond_b_f1': _L0_cond_in['b_f1'], 'L0_cond_w_f2': _L0_cond_in['w_f2'], 'L0_cond_b_f2': _L0_cond_in['b_f2'], 'L0_cond_w_ada': _L0_cond_in['w_ada'], 'L0_cond_b_ada': _L0_cond_in['b_ada'], 'L1_cond_Wx': _L1_cond_in['Wx'], 'L1_cond_Wh': _L1_cond_in['Wh'], 'L1_cond_b': _L1_cond_in['b']}

def reference(x, cond_1024, L0_cond_w_q, L0_cond_b_q, L0_cond_w_k, L0_cond_b_k, L0_cond_w_v, L0_cond_b_v, L0_cond_w_o, L0_cond_b_o, L0_cond_w_f1, L0_cond_b_f1, L0_cond_w_f2, L0_cond_b_f2, L0_cond_w_ada, L0_cond_b_ada, L1_cond_Wx, L1_cond_Wh, L1_cond_b):
    import jax
    import jax.numpy as jnp

    def _L0_cond_ref(x, t_emb, w_q, b_q, w_k, b_k, w_v, b_v, w_o, b_o, w_f1, b_f1, w_f2, b_f2, w_ada, b_ada):
        import math
        import jax, jax.numpy as jnp
        import numpy as np
        EPS = 1e-07
        MAX_TANH_ARG = 1.0 - 1e-05

        def _norm(x):
            return jnp.sqrt(jnp.sum(x * x, axis=-1, keepdims=True)).clip(EPS)

        def logmap0(x):
            n = _norm(x)
            return jnp.arctanh(jnp.clip(n, EPS, MAX_TANH_ARG)) * x / n

        def expmap0(v):
            n = _norm(v)
            return jnp.tanh(n) * v / n

        def mobius_add(x, y):
            x2 = jnp.sum(x * x, -1, keepdims=True)
            y2 = jnp.sum(y * y, -1, keepdims=True)
            xy = jnp.sum(x * y, -1, keepdims=True)
            num = (1 + 2 * xy + y2) * x + (1 - x2) * y
            den = (1 + 2 * xy + x2 * y2).clip(EPS)
            return num / den

        def plin(x, w, b):
            return expmap0(logmap0(x) @ w + b)

        def layer_norm(x, eps=1e-06):
            m = x.mean(-1, keepdims=True)
            v = ((x - m) ** 2).mean(-1, keepdims=True)
            return (x - m) / jnp.sqrt(v + eps)

        def _beta(a, b):
            return math.exp(math.lgamma(a) + math.lgamma(b) - math.lgamma(a + b))
        D, H, FF = (256, 16, 1024)
        HD = D // H
        BETA_N = _beta(D / 2, 0.5)
        BETA_H = _beta(HD / 2, 0.5)

        def _to_heads(p):
            B, S, _ = p.shape
            t = logmap0(p).reshape(B, S, H, HD) * (BETA_H / BETA_N)
            return expmap0(jnp.transpose(t, (0, 2, 1, 3)))

        def _from_heads(ph):
            B, _, S, _ = ph.shape
            t = logmap0(ph) * (BETA_N / BETA_H)
            t = jnp.transpose(t, (0, 2, 1, 3)).reshape(B, S, D)
            return expmap0(t)
        ada = t_emb @ w_ada + b_ada
        sh_msa, sc_msa, g_msa, sh_mlp, sc_mlp, g_mlp = jnp.split(ada, 6, axis=-1)
        residual = x
        xn = layer_norm(logmap0(x))
        xm = expmap0(xn * (1 + sc_msa) + sh_msa)
        q = _to_heads(plin(xm, w_q, b_q))
        k = _to_heads(plin(xm, w_k, b_k))
        v = _to_heads(plin(xm, w_v, b_v))
        qt, kt, vt = (logmap0(q), logmap0(k), logmap0(v))
        scores = jnp.einsum('bhqd,bhkd->bhqk', qt, kt) / math.sqrt(HD)
        attn = jax.nn.softmax(scores, axis=-1)
        out_h = expmap0(jnp.einsum('bhqk,bhkd->bhqd', attn, vt))
        attn_out = plin(_from_heads(out_h), w_o, b_o)
        attn_t = g_msa * logmap0(attn_out)
        x = mobius_add(residual, expmap0(attn_t))
        residual = x
        xn = layer_norm(logmap0(x))
        xm = expmap0(xn * (1 + sc_mlp) + sh_mlp)
        ff = plin(plin(xm, w_f1, b_f1), w_f2, b_f2)
        ff_t = g_mlp * logmap0(ff)
        return mobius_add(residual, expmap0(ff_t))

    def _L1_cond_ref(x, h0, Wx, Wh, b):
        import jax, jax.numpy as jnp
        import numpy as np
        N, T, D, H = (64, 64, 256, 256)
        xW = jnp.einsum('ntd,dh->nth', x, Wx) + b

        def step(prev_h, xw_t):
            next_h = jnp.tanh(xw_t + prev_h @ Wh)
            return (next_h, next_h)
        _, hs = jax.lax.scan(step, h0, jnp.swapaxes(xW, 0, 1))
        return jnp.swapaxes(hs, 0, 1)
    x = x + _L0_cond_ref(x, cond_1024[:, None, :], L0_cond_w_q, L0_cond_b_q, L0_cond_w_k, L0_cond_b_k, L0_cond_w_v, L0_cond_b_v, L0_cond_w_o, L0_cond_b_o, L0_cond_w_f1, L0_cond_b_f1, L0_cond_w_f2, L0_cond_b_f2, L0_cond_w_ada, L0_cond_b_ada)
    x = x + _L1_cond_ref(x, cond_1024, L1_cond_Wx, L1_cond_Wh, L1_cond_b)
    return x

_drawn_inputs = setup_inputs


def setup_inputs(seed=0):
    import zlib

    import numpy as np

    out = dict(_drawn_inputs(seed))
    spreads = {'L0_cond_b_q': (0.0, 2.0),
     'L0_cond_b_k': (0.0, 2.0),
     'L0_cond_b_v': (0.0, 0.1),
     'L0_cond_b_o': (0.0, 0.1),
     'L0_cond_b_f1': (0.0, 0.1),
     'L0_cond_b_f2': (0.0, 0.1),
     'L0_cond_b_ada': (0.0, 0.1),
     'L1_cond_b': (0.0, 0.1)}
    factors = {'L0_cond_w_q': 110.105, 'L0_cond_w_k': 64.415}
    for name, (base, spread) in spreads.items():
        noise = np.random.default_rng([zlib.crc32(name.encode()), seed]).standard_normal(out[name].shape)
        drawn = base * np.exp(spread * noise) if base else spread * noise
        out[name] = jnp.asarray(drawn.astype(out[name].dtype))
    for name, factor in factors.items():
        out[name] = (out[name] * factor).astype(out[name].dtype)
    return out
```

```python
import math
from contextlib import ExitStack

import numpy as np

import concourse.bass as bass
from concourse import mybir

F32 = mybir.dt.float32
BF16 = mybir.dt.bfloat16
I32 = mybir.dt.int32
ALU = mybir.AluOpType
ACT = mybir.ActivationFunctionType
AX_X = mybir.AxisListType.X

P = 128
B, S, D = 2, 1024, 256
H, HD, FF = 16, 16, 1024
TOK = P // B
TILES = S // TOK
DC = D // P
FC = FF // P
KC = S // P
PARTS = 6
QUAD = 4
HG = H // QUAD
BLK = 16

EPS = 1e-7
MAXN = float(np.float32(1.0 - 1e-05))
RADIUS = math.atanh(MAXN)
TINY = 1e-30


def _beta(a, b):
    return math.exp(math.lgamma(a) + math.lgamma(b) - math.lgamma(a + b))


BETA_N = _beta(D / 2, 0.5)
BETA_H = _beta(HD / 2, 0.5)
RHO = BETA_H / BETA_N
ONE_BITS = float(127 << 23)
LOG_STEP = 0.5 * math.log(2.0) * 2.0 ** -23
MAGIC = float(0x5F3759DF)


def build(nc, x, cond, w_q, b_q, w_k, b_k, w_v, b_v, w_o, b_o, w_f1, b_f1, w_f2, b_f2, w_ada, b_ada,
          w_x, w_h, b_h, out):
    with ExitStack() as ctx:
        def sb(name, shape, dt=F32):
            return ctx.enter_context(nc.sbuf_tensor(name, shape, dt))

        def sem(name):
            return ctx.enter_context(nc.semaphore(name))

        kT = sb("kT", [96, H, B, S], BF16)
        vals = sb("vals", [P, KC, B, H, HD + 1])
        xp_buf = sb("xp_buf", [P, TILES * D])
        x_all = xp_buf[:].rearrange("p (i d) -> p i d", d=D)
        probs = xp_buf[:].rearrange("p (g j n) -> p g j n", g=2, j=QUAD)
        qf = sb("qf", [P, TILES, D])
        wada_sb = qf[:].rearrange("p i d -> p (i d)")[:, 0:DC * 6 * D].rearrange("p (c n) -> p c n", c=DC)
        wo = sb("wo", [P, DC, D])
        wf1 = sb("wf1", [P, DC, FF])
        wf2 = sb("wf2", [P, FC, D])
        wx = sb("wx", [P, DC, D])
        wh = sb("wh", [P, 2, D])
        perm = sb("perm", [P, 2, D])
        bh_row = sb("bh_row", [1, D])
        mod = sb("mod", [P, 6 * D])
        bo = sb("bo", [P, D])
        bf1 = sb("bf1", [P, FF])
        bf2 = sb("bf2", [P, D])
        bada_row = kT[0:1].rearrange("p h b s -> p (h b s)").bitcast(F32)[:, 0:6 * D]
        condT = sb("condT", [P, DC, B])
        cond_rows = sb("cond_rows", [P, DC, P])
        ident = sb("ident", [P, P])
        ident_bf = sb("ident_bf", [P, P], BF16)
        tiny = sb("tiny", [P, 1])
        ones_row = sb("ones_row", [1, P])
        halves = sb("halves", [P, 2, TILES])
        hist = sb("hist", [P, 2, (TOK + 1) * 32])
        xT = sb("xT", [P, DC, P])
        scal = sb("scal", [P, 40, TILES])
        alpha_all = sb("alpha_all", [P, TILES])
        beta_all = sb("beta_all", [P, TILES])
        resid = sb("resid", [P, D])
        work = sb("work", [P, 22 * D])

        def carve(*sizes):
            at, parts = 0, []
            for n in sizes:
                parts.append(work[:, at:at + n])
                at += n
            return parts

        wqkv, t1, t1T, y, ysq, kf, junk_p, bqkv = carve(DC * 3 * D, 2 * D, 2 * D, 3 * D, 3 * D, D, 2 * D, 3 * D)
        wqkv = wqkv.rearrange("p (c n) -> p c n", c=DC)
        t1 = t1.rearrange("p (e d) -> p e d", e=2)
        t1T = t1T.rearrange("p (e c t) -> p e c t", e=2, c=DC)
        oT, y1, y1T, junk_a, xin, wa, wb, junk_v, x1, xo, aT, oat = carve(2 * D, FF, FF, FF, D, D, D, D, D, D, D, D)
        y1T = y1T.rearrange("p (c t) -> p c t", c=FC)
        aT = aT.rearrange("p (c t) -> p c t", c=DC)
        stackb = sb("stackb", [P, H, PARTS, HD], BF16)
        qT = sb("qT", [96, H, P], BF16)
        nw = sb("nw", [P, 4, 3 * H + 3])
        fac = sb("fac", [P, 3, H])
        fac3 = sb("fac3", [P, 3])
        c1 = sb("c1", [P, 2])
        ss1 = sb("ss1", [P, 2])
        c1t = sb("c1t", [P, 2])
        bns = sb("bns", [P, 6])
        bna = sb("bna", [P, TILES, 2])

        bank = [ctx.enter_context(nc.psum_tensor(f"bank{n}", [P, 512], F32)) for n in range(8)]
        z_bank = bank[0:2]
        s_bank = bank[2:6]
        o_bank = bank[6]
        m_bank = bank[7]

        names = """x_in w_in b_in cond_in gconst gmem ada_done cond_spread mod_done
            st_v st_g st_a st_n xn_a t1_v ss_a c1_g t1_pe t1T_a qkv_pe y_v sq_a f_v
            k1_a r1_v k2_a k3_v kst_pe kev_a kev_v v_v h0_in
            qr_v q1_a q2_a q3_v qst_pe qev_a qev_v s_pe p_a pv_pe
            o_ev to_pe osq_a of_v zt_v oss_g z_pe zc_a wo_pe yo_v yo2_a co_g w_v w2_a wx_v mob_g x1_v bn_v
            th_a th_g th2_a th3_g ln_g xn2_a t2_v t2s_a c2_g t2_pe t2T_a f1_pe y1_v y1s_a c3_g y1_pe y1T_a f2_pe
            y2_v y2s_a c4_g w2_v w22_a w2x_v tm_g tm_a mob2_g xo_v xo_pe xT_a xin_in
            z_pe_step tr_v h_a flush_pe out_v out_dma""".split()
        s = {n: sem(n) for n in names}
        dve_link, pool_link, act_link = sem("dve_link"), sem("pool_link"), sem("act_link")
        block = ctx.enter_context(nc.Block())

        def chain(eng, link_sem):
            count = [0]

            def link(ins):
                count[0] += 1
                ins.then_inc(link_sem, 1)
                eng.wait_ge(link_sem, count[0])

            def restart():
                eng.sem_clear(link_sem)
                count[0] = 0
            return link, restart

        def rows_of(v):
            return v.rearrange("(a n) -> a n", a=1)

        @block.sync
        def _(sp):
            for b in range(B):
                for h in range(2):
                    src = x[b].rearrange("(i t) d -> t i d", t=TOK)
                    sp.dma_start(x_all[b * TOK:(b + 1) * TOK, 8 * h:8 * h + 8, :],
                                 src[:, 8 * h:8 * h + 8, :]).then_inc(s["x_in"], 16)
            for n, w in enumerate((w_q, w_k, w_v)):
                sp.dma_start(wqkv[:, :, n * D:(n + 1) * D],
                             w.rearrange("(c p) n -> p c n", p=P)).then_inc(s["w_in"], 16)
            for dst, w in ((wo, w_o), (wf1, w_f1), (wf2, w_f2), (wx, w_x)):
                sp.dma_start(dst[:], w.rearrange("(c p) n -> p c n", p=P)).then_inc(s["w_in"], 16)
            whv = w_h.rearrange("(j c p) n -> j p c n", c=2, p=32)
            for j in range(QUAD):
                sp.dma_start(wh[32 * j:32 * j + 32, :, :], whv[j]).then_inc(s["w_in"], 16)

            def tile_in(i):
                for b in range(B):
                    sp.dma_start(xin[b * TOK:(b + 1) * TOK, :],
                                 x[b, bass.ds(i * TOK, TOK), :]).then_inc(s["xin_in"], 16)

            def tile_out(i):
                for b in range(B):
                    sp.dma_start(out[b, bass.ds(i * TOK, TOK), :],
                                 oat[b * TOK:(b + 1) * TOK, :]).then_inc(s["out_dma"], 16)

            sp.wait_ge(s["kev_v"], TILES)
            with sp.Fori(0, TILES) as i:
                sp.wait_ge(s["xo_v"], i)
                tile_in(i)
                sp.wait_ge(s["out_v"], i + 1)
                tile_out(i)
            sp.wait_ge(s["out_dma"], 32 * TILES)

        @block.gpsimd
        def _(pool):
            g = nc.gpsimd
            link, restart = chain(pool, pool_link)
            g.memset(tiny[:], TINY).then_inc(s["gconst"], 1)
            g.memset(ones_row[:], 1.0).then_inc(s["gconst"], 1)
            g.memset(halves[:, 0, :], 0.5).then_inc(s["gconst"], 1)
            g.memset(halves[:, 1, :], -0.5).then_inc(s["gconst"], 1)
            link(g.memset(ident[:], 0.0))
            g.affine_select(out=ident[:], in_=ident[:], compare_op=ALU.not_equal, fill=1.0, base=0,
                            pattern=[[-1, P]], channel_multiplier=1).then_inc(s["gconst"], 1)
            g.memset(perm[:], 0.0).then_inc(s["gmem"], 1)
            g.memset(vals[:], 1.0).then_inc(s["gmem"], 1)
            g.memset(hist[:], 0.0).then_inc(s["gmem"], 1)
            pool.wait_ge(s["gconst"], 5)

            def power(dst, src, half, n):
                link(g.tensor_tensor(dst, src, halves[:, half, 0:n], ALU.pow))

            def sc(k, n=1):
                return scal[:, k, 0:n]

            def log_a(mean, var, n):
                link(g.tensor_tensor(sc(0, n), mean, mean, ALU.mult))
                link(g.tensor_tensor(sc(0, n), sc(0, n), var, ALU.add))
                link(g.tensor_scalar(sc(1, n), sc(0, n), float(D), 0.0, ALU.mult, ALU.max))
                power(sc(2, n), sc(1, n), 0, n)
                link(g.tensor_scalar(sc(2, n), sc(2, n), EPS, None, ALU.max))
                link(g.tensor_scalar(sc(3, n), sc(2, n), MAXN, None, ALU.min))

            def log_b(mean, var, alpha, beta, n):
                link(g.tensor_tensor(sc(9, n), sc(8, n), sc(8, n), ALU.mult))
                link(g.tensor_scalar(sc(10, n), sc(9, n), 0.2, 1.0 / 3.0, ALU.mult, ALU.add))
                link(g.tensor_tensor(sc(10, n), sc(10, n), sc(9, n), ALU.mult))
                link(g.tensor_scalar(sc(10, n), sc(10, n), 1.0, 1.0, ALU.mult, ALU.add))
                link(g.tensor_tensor(sc(10, n), sc(10, n), sc(8, n), ALU.mult))
                link(g.tensor_tensor(sc(10, n), sc(10, n), sc(5, n), ALU.add))
                link(g.tensor_tensor(sc(11, n), sc(10, n), sc(13, n), ALU.mult))
                link(g.tensor_tensor(sc(12, n), sc(11, n), sc(11, n), ALU.mult))
                link(g.tensor_tensor(sc(12, n), sc(12, n), var, ALU.mult))
                link(g.tensor_scalar(sc(12, n), sc(12, n), 1e-6, 0.0, ALU.add, ALU.max))
                power(sc(14, n), sc(12, n), 1, n)
                link(g.tensor_tensor(alpha, sc(14, n), sc(11, n), ALU.mult))
                link(g.tensor_tensor(sc(15, n), alpha, mean, ALU.mult))
                return g.tensor_scalar(beta, sc(15, n), -1.0, 0.0, ALU.mult, ALU.add)

            def clip(dst, src, tmp, factor=RADIUS):
                link(g.tensor_tensor(tmp, src, tiny[:], ALU.add))
                power(tmp, tmp, 1, 1)
                return g.tensor_scalar(dst, tmp, factor, 1.0, ALU.mult, ALU.min)

            pool.wait_ge(s["st_v"], 1)
            log_a(bna[:, :, 0], bna[:, :, 1], TILES)
            g.tensor_copy(sc(16, TILES), sc(3, TILES)).then_inc(s["st_g"], 1)
            pool.wait_ge(s["st_n"], 2)
            log_b(bna[:, :, 0], bna[:, :, 1], alpha_all[:], beta_all[:], TILES).then_inc(s["st_g"], 1)

            with pool.Fori(0, TILES // 2) as m:
                restart()
                for e in range(2):
                    pool.wait_ge(s["ss_a"], 2 * m + e + 1)
                    clip(c1[:, e:e + 1], ss1[:, e:e + 1], c1t[:, e:e + 1]).then_inc(s["c1_g"], 1)

            def mobius(n_tanh, ss_w, dot, ss_x, p_out, q_out, tm_g, tm_a, i1):
                power(sc(20), ss_w, 0, 1)
                link(g.tensor_scalar(sc(20), sc(20), EPS, None, ALU.max))
                power(sc(22), sc(20), 1, 1)
                g.tensor_tensor(sc(22), sc(22), sc(22), ALU.mult).then_inc(tm_g, 1)
                pool.wait_ge(tm_a, i1)
                link(g.tensor_tensor(sc(23), sc(21), sc(22), ALU.mult))
                link(g.tensor_tensor(sc(24), sc(23), sc(23), ALU.mult))
                link(g.tensor_tensor(sc(24), sc(24), ss_w, ALU.mult))
                link(g.tensor_tensor(sc(25), sc(23), dot, ALU.mult))
                link(g.tensor_scalar(sc(26), sc(25), 2.0, 1.0, ALU.mult, ALU.add))
                link(g.tensor_tensor(sc(27), sc(26), sc(24), ALU.add))
                link(g.tensor_tensor(sc(28), ss_x, sc(24), ALU.mult))
                link(g.tensor_tensor(sc(28), sc(28), sc(26), ALU.add))
                link(g.tensor_scalar(sc(28), sc(28), EPS, None, ALU.max))
                power(sc(29), sc(28), 1, 1)
                link(g.tensor_tensor(sc(29), sc(29), sc(29), ALU.mult))
                link(g.tensor_tensor(p_out, sc(27), sc(29), ALU.mult))
                link(g.tensor_scalar(sc(30), ss_x, -1.0, 1.0, ALU.mult, ALU.add))
                link(g.tensor_tensor(sc(30), sc(30), sc(29), ALU.mult))
                return g.tensor_tensor(q_out, sc(30), sc(23), ALU.mult)

            def post(i):
                i1 = i + 1
                restart()
                pool.wait_ge(s["of_v"], i1)
                clip(scal[:, 31, 1:2], scal[:, 31, 0:1], scal[:, 31, 2:3]).then_inc(s["oss_g"], 1)
                pool.wait_ge(s["yo2_a"], i1)
                clip(scal[:, 32, 1:2], scal[:, 32, 0:1], scal[:, 32, 2:3]).then_inc(s["co_g"], 1)
                pool.wait_ge(s["w2_a"], i1)
                pool.wait_ge(s["wx_v"], i1)
                mobius(sc(21), scal[:, 33, 0:1], scal[:, 33, 1:2], scal[:, 33, 2:3],
                       scal[:, 34, 0:1], scal[:, 34, 1:2], s["tm_g"], s["tm_a"], 2 * i + 1)\
                    .then_inc(s["mob_g"], 1)
                pool.wait_ge(s["bn_v"], i1)
                log_a(scal[:, 35, 0:1], scal[:, 35, 1:2], 1)
                g.tensor_copy(sc(16), sc(3)).then_inc(s["th_g"], 1)
                pool.wait_ge(s["th3_g"], i1)
                log_b(scal[:, 35, 0:1], scal[:, 35, 1:2], scal[:, 36, 0:1], scal[:, 36, 1:2], 1)\
                    .then_inc(s["ln_g"], 1)
                pool.wait_ge(s["t2s_a"], i1)
                clip(scal[:, 37, 1:2], scal[:, 37, 0:1], scal[:, 37, 2:3]).then_inc(s["c2_g"], 1)
                pool.wait_ge(s["y1s_a"], i1)
                clip(scal[:, 38, 1:2], scal[:, 38, 0:1], scal[:, 38, 2:3]).then_inc(s["c3_g"], 1)
                pool.wait_ge(s["y2s_a"], i1)
                clip(scal[:, 39, 1:2], scal[:, 39, 0:1], scal[:, 39, 2:3]).then_inc(s["c4_g"], 1)
                pool.wait_ge(s["w22_a"], i1)
                pool.wait_ge(s["w2x_v"], i1)
                mobius(sc(21), scal[:, 33, 3:4], scal[:, 33, 4:5], sc(1),
                       scal[:, 34, 2:3], scal[:, 34, 3:4], s["tm_g"], s["tm_a"], 2 * i + 2)\
                    .then_inc(s["mob2_g"], 1)

            with pool.Fori(0, TILES) as i:
                post(i)

        @block.scalar
        def _(act):
            a = nc.scalar
            for n, bvec in enumerate((b_q, b_k, b_v)):
                act.dma_start(bqkv[:, n * D:(n + 1) * D], rows_of(bvec).broadcast_to([P, D])).then_inc(s["b_in"], 16)
            for c in range(DC):
                act.dma_start(wada_sb[:, c, :], w_ada[c * P:(c + 1) * P, :]).then_inc(s["cond_in"], 16)
            for c in range(DC):
                act.dma_start(condT[:, c, :], cond[:, c * P:(c + 1) * P].rearrange("b p -> p b"),
                              allow_slow_non_contiguous=True).then_inc(s["cond_in"], 16)
            act.dma_start(bada_row[:], rows_of(b_ada)).then_inc(s["cond_in"], 16)
            for dst, bvec, n in ((bo, b_o, D), (bf1, b_f1, FF), (bf2, b_f2, D)):
                act.dma_start(dst[:], rows_of(bvec).broadcast_to([P, n])).then_inc(s["b_in"], 16)
            act.dma_start(bh_row[:], rows_of(b_h)).then_inc(s["b_in"], 16)
            act.wait_ge(s["gmem"], 3)
            hv = cond.rearrange("b (j c p) -> j c p b", c=2, p=32)
            for j in range(QUAD):
                for c in range(2):
                    act.dma_start(hist[32 * j:32 * j + 32, c, 32 * TOK:32 * TOK + B], hv[j, c],
                                  allow_slow_non_contiguous=True).then_inc(s["h0_in"], 16)
            act.wait_ge(s["st_v"], 2)
            a.activation(scal[:, 6, :], scal[:, 5, :], ACT.Tanh).then_inc(s["st_a"], 1)

            with act.Fori(0, TILES // 2) as m:
                for e in range(2):
                    n1 = 2 * m + e + 1
                    if e == 0:
                        act.wait_ge(s["st_g"], 2)
                        act.wait_ge(s["t1_pe"], 2 * m)
                    a.activation(t1[:, e, :], x_all[:, bass.ds(2 * m + e, 1), :].rearrange("p a d -> p (a d)"), ACT.Identity,
                                 bias=beta_all[:, bass.ds(2 * m + e, 1)],
                                 scale=alpha_all[:, bass.ds(2 * m + e, 1)]).then_inc(s["xn_a"], 1)
                for e in range(2):
                    n1 = 2 * m + e + 1
                    act.wait_ge(s["t1_v"], n1)
                    if e == 0:
                        act.wait_ge(s["y_v"], 2 * m)
                    a.activation(junk_p[:, e * D:(e + 1) * D], t1[:, e, :], ACT.Square,
                                 accum_out=ss1[:, e:e + 1]).then_inc(s["ss_a"], 1)
                    act.wait_ge(s["t1_pe"], n1)
                    a.activation(t1T[:, e, :, :], bank[0][:, e * D:(e + 1) * D].rearrange("p (c t) -> p c t", c=DC),
                                 ACT.Copy).then_inc(s["t1T_a"], 1)
                    act.wait_ge(s["y_v"], n1)
                    a.activation(ysq[:], y[:], ACT.Square).then_inc(s["sq_a"], 1)
                    act.wait_ge(s["f_v"], n1)
                    if e == 0:
                        act.wait_ge(s["kst_pe"], 4 * m)
                    else:
                        act.wait_ge(s["kst_pe"], 4 * m + 2)
                    k_h = kf[:].rearrange("p (h o d) -> p h o d", h=H, o=1)
                    a.activation(stackb[:, :, 0:3, :], k_h.broadcast_to([P, H, 3, HD]), ACT.Copy).then_inc(s["k1_a"], 1)
                    act.wait_ge(s["r1_v"], n1)
                    r_h = resid[:].rearrange("p (h o d) -> p h o d", h=H, o=1)
                    a.activation(stackb[:, :, 3:5, :], r_h.broadcast_to([P, H, 2, HD]), ACT.Copy).then_inc(s["k2_a"], 1)
                    act.wait_ge(s["kst_pe"], 4 * m + 2 * e + 1)
                    a.activation(kT[:, 0:8, :, bass.ds((2 * m + e) * TOK, TOK)],
                                 bank[3][:].bitcast(BF16)[0:96, :].rearrange("p (h b t) -> p h b t", h=8, b=B),
                                 ACT.Copy).then_inc(s["kev_a"], 1)

            def att(i):
                i1 = i + 1
                q_h = qf[:, bass.ds(i, 1), :].rearrange("p a (h o d) -> p (a h) o d", h=H, o=1)
                act.wait_ge(s["qst_pe"], 2 * i)
                a.activation(stackb[:, :, 0:4:3, :], q_h.broadcast_to([P, H, 2, HD]), ACT.Copy)
                a.activation(stackb[:, :, 5:6, :], q_h, ACT.Copy).then_inc(s["q1_a"], 1)
                act.wait_ge(s["qr_v"], i1)
                r_h = resid[:].rearrange("p (h o d) -> p h o d", h=H, o=1)
                a.activation(stackb[:, :, 1:5:3, :], r_h.broadcast_to([P, H, 2, HD]), ACT.Copy).then_inc(s["q2_a"], 1)
                act.wait_ge(s["qst_pe"], 2 * i + 1)
                act.wait_ge(s["s_pe"], 32 * i)
                a.activation(qT[:, 0:8, :], bank[3][:].bitcast(BF16)[0:96, :].rearrange("p (h t) -> p h t", h=8),
                             ACT.Copy).then_inc(s["qev_a"], 1)
                for u in range(32):
                    gb, j = u // 4, u % 4
                    act.wait_ge(s["s_pe"], 32 * i + u + 1)
                    if j == 0:
                        if gb >= 2:
                            act.wait_ge(s["pv_pe"], 8 * i + gb - 1)
                        else:
                            act.wait_ge(s["pv_pe"], 8 * i)
                    a.activation(probs[:, gb % 2, j, :], s_bank[u % 4][:, :], ACT.Exp).then_inc(s["p_a"], 1)

            def post(i):
                i1 = i + 1
                act.wait_ge(s["pv_pe"], 8 * i + 8)
                a.activation(oT[:], o_bank[:, :], ACT.Copy).then_inc(s["o_ev"], 1)
                act.wait_ge(s["to_pe"], i1)
                to = s_bank[0][:].rearrange("p (h r) -> p h r", h=H)
                a.activation(junk_a[:, 0:D].rearrange("p (h d) -> p h d", h=H), to[:, :, 0:HD], ACT.Square)\
                    .then_inc(s["osq_a"], 1)
                act.wait_ge(s["z_pe"], i1)
                a.activation(aT[:], m_bank[:, 0:D].rearrange("p (c t) -> p c t", c=DC), ACT.Copy).then_inc(s["zc_a"], 1)
                act.wait_ge(s["xin_in"], 32 * i + 32)
                a.activation(junk_a[:, 256:512], xin[:], ACT.Square, accum_out=scal[:, 33, 2:3])
                act.wait_ge(s["yo_v"], i1)
                a.activation(junk_a[:, 512:768], wa[:], ACT.Square, accum_out=scal[:, 32, 0:1]).then_inc(s["yo2_a"], 1)
                act.wait_ge(s["w_v"], i1)
                a.activation(junk_a[:, 768:1024], wb[:], ACT.Square, accum_out=scal[:, 33, 0:1]).then_inc(s["w2_a"], 1)
                act.wait_ge(s["tm_g"], 2 * i + 1)
                a.activation(scal[:, 21, 0:1], scal[:, 20, 0:1], ACT.Tanh).then_inc(s["tm_a"], 1)
                act.wait_ge(s["th_a"], i1)
                a.activation(scal[:, 6, 0:1], scal[:, 5, 0:1], ACT.Tanh).then_inc(s["th2_a"], 1)
                act.wait_ge(s["ln_g"], i1)
                a.activation(wa[:], x1[:], ACT.Identity, bias=scal[:, 36, 1:2], scale=scal[:, 36, 0:1])\
                    .then_inc(s["xn2_a"], 1)
                act.wait_ge(s["t2_v"], i1)
                a.activation(junk_a[:, 0:256], wb[:], ACT.Square, accum_out=scal[:, 37, 0:1]).then_inc(s["t2s_a"], 1)
                act.wait_ge(s["t2_pe"], i1)
                a.activation(aT[:], m_bank[:, 0:D].rearrange("p (c t) -> p c t", c=DC), ACT.Copy).then_inc(s["t2T_a"], 1)
                act.wait_ge(s["y1_v"], i1)
                a.activation(junk_a[:], y1[:], ACT.Square, accum_out=scal[:, 38, 0:1]).then_inc(s["y1s_a"], 1)
                act.wait_ge(s["y1_pe"], 2 * i + 1)
                a.activation(y1T[:, 0:4, :], s_bank[2][:].rearrange("p (c t) -> p c t", c=4), ACT.Copy)
                act.wait_ge(s["y1_pe"], 2 * i + 2)
                a.activation(y1T[:, 4:8, :], s_bank[3][:].rearrange("p (c t) -> p c t", c=4), ACT.Copy)\
                    .then_inc(s["y1T_a"], 1)
                act.wait_ge(s["y2_v"], i1)
                a.activation(junk_a[:, 256:512], wa[:], ACT.Square, accum_out=scal[:, 39, 0:1]).then_inc(s["y2s_a"], 1)
                act.wait_ge(s["w2_v"], i1)
                a.activation(junk_a[:, 512:768], wb[:], ACT.Square, accum_out=scal[:, 33, 3:4]).then_inc(s["w22_a"], 1)
                act.wait_ge(s["tm_g"], 2 * i + 2)
                a.activation(scal[:, 21, 0:1], scal[:, 20, 0:1], ACT.Tanh).then_inc(s["tm_a"], 1)
                act.wait_ge(s["xo_pe"], i1)
                a.activation(xT[:].rearrange("p c (t b) -> p c b t", b=B),
                             m_bank[:, 0:D].rearrange("p (c b t) -> p c b t", c=DC, b=B), ACT.Copy).then_inc(s["xT_a"], 1)

            def rnn_step(i, t):
                m = t % BLK
                z = z_bank[(t // BLK) % 2]
                act.wait_ge(s["tr_v"], i * TOK + t + 1)
                a.activation(hist[:, :, 32 * (t + 1) + 0:32 * (t + 1) + B],
                             z[:, 64:128].rearrange("p (c r) -> p c r", c=2)[:, :, 2 * m:2 * m + B],
                             ACT.Tanh).then_inc(s["h_a"], 1)

            act.wait_ge(s["kst_pe"], 2 * TILES)
            with act.Fori(0, TILES) as i:
                att(i)
                post(i)
                for t in range(TOK):
                    rnn_step(i, t)

        @block.vector
        def _(dve):
            v = nc.vector
            link, restart = chain(dve, dve_link)
            restart()
            dve.wait_ge(s["gmem"], 3)
            dve.wait_ge(s["gconst"], 5)
            v.tensor_copy(ident_bf[:], ident[:]).then_inc(s["cond_spread"], 1)
            for j in range(QUAD):
                for c in range(2):
                    o = 64 * j + 32 * c
                    v.tensor_copy(perm[32 * j:32 * j + 32, c, o:o + 32],
                                  ident[32 * j:32 * j + 32, 32 * j:32 * j + 32]).then_inc(s["cond_spread"], 1)
            dve.wait_ge(s["cond_in"], 80)
            for c in range(DC):
                for b in range(B):
                    v.tensor_scalar(cond_rows[:, c, b * TOK:(b + 1) * TOK], ident[:, 0:TOK], 0.0, condT[:, c, b:b + 1],
                                    ALU.mult, ALU.add).then_inc(s["cond_spread"], 1)
            dve.wait_ge(s["x_in"], 64)
            link(v.memset(o_bank[:, :], 0.0))
            for i in range(TILES):
                link(v.bn_stats(bns[:], x_all[:, i, :]))
                link(v.bn_aggr(bna[:, i, :], bns[:]))
            v.engine_nop().then_inc(s["st_v"], 1)

            dve.wait_ge(s["ada_done"], 1)
            for n in range(3):
                v.tensor_copy(mod[:, n * 512:(n + 1) * 512], bank[n][:, :]).then_inc(s["mod_done"], 1)
            dve.wait_ge(s["mod_done"], 3)
            for n in (1, 4):
                v.tensor_scalar(mod[:, n * D:(n + 1) * D], mod[:, n * D:(n + 1) * D], 1.0, None, ALU.add)\
                    .then_inc(s["mod_done"], 1)
            dve.wait_ge(s["mod_done"], 5)

            def sc(k, n=1):
                return scal[:, k, 0:n]

            def guess(n):
                link(v.tensor_scalar(sc(4, n), sc(16, n), -1.0, 1.0, ALU.mult, ALU.add))
                link(v.reciprocal(sc(4, n), sc(4, n)))
                link(v.scalar_tensor_tensor(sc(4, n), sc(16, n), 1.0, sc(4, n), ALU.add, ALU.mult))
                return v.tensor_scalar(sc(5, n), sc(4, n).bitcast(I32), ONE_BITS, LOG_STEP, ALU.subtract, ALU.mult)

            def correct(n):
                link(v.tensor_tensor(sc(7, n), sc(16, n), sc(6, n), ALU.mult))
                link(v.tensor_scalar(sc(7, n), sc(7, n), -1.0, 1.0, ALU.mult, ALU.add))
                link(v.reciprocal(sc(7, n), sc(7, n)))
                link(v.tensor_tensor(sc(8, n), sc(16, n), sc(6, n), ALU.subtract))
                link(v.tensor_tensor(sc(8, n), sc(8, n), sc(7, n), ALU.mult))
                return v.reciprocal(sc(13, n), sc(2, n))

            dve.wait_ge(s["st_g"], 1)
            guess(TILES).then_inc(s["st_v"], 1)
            dve.wait_ge(s["st_a"], 1)
            correct(TILES).then_inc(s["st_n"], 2)

            def rsqrt(y_, x_, t_, bits):
                link(v.tensor_scalar(bits, x_.bitcast(I32), 1, None, ALU.logical_shift_right))
                link(v.tensor_scalar(y_.bitcast(I32), bits, -1.0, MAGIC, ALU.mult, ALU.add))
                for _ in range(3):
                    link(v.scalar_tensor_tensor(t_, y_, -0.5, y_, ALU.mult, ALU.mult))
                    link(v.tensor_tensor(t_, t_, x_, ALU.mult))
                    link(v.scalar_tensor_tensor(y_, t_, 1.5, y_, ALU.add, ALU.mult))

            N = 3 * H
            with dve.Fori(0, TILES // 2) as m:
                restart()
                for e in range(2):
                    n1 = 2 * m + e + 1
                    dve.wait_ge(s["xn_a"], n1)
                    link(v.tensor_tensor(t1[:, e, :], t1[:, e, :], mod[:, D:2 * D], ALU.mult))
                    v.tensor_tensor(t1[:, e, :], t1[:, e, :], mod[:, 0:D], ALU.add).then_inc(s["t1_v"], 1)
                for e in range(2):
                    n1 = 2 * m + e + 1
                    dve.wait_ge(s["c1_g"], n1)
                    dve.wait_ge(s["qkv_pe"], n1)
                    dve.wait_ge(s["b_in"], 16 * 7)
                    v.scalar_tensor_tensor(y[:, 0:512], bank[1][:, :], c1[:, e:e + 1], bqkv[:, 0:512],
                                           ALU.mult, ALU.add)
                    v.scalar_tensor_tensor(y[:, 512:768], bank[2][:, 0:D], c1[:, e:e + 1], bqkv[:, 512:768],
                                           ALU.mult, ALU.add).then_inc(s["y_v"], 1)
                    dve.wait_ge(s["sq_a"], n1)
                    link(v.tensor_reduce(nw[:, 0, 0:N], ysq[:].rearrange("p (h d) -> p h d", d=HD), AX_X, ALU.add))
                    link(v.tensor_reduce(nw[:, 0, N:N + 3], nw[:, 0, 0:N].rearrange("p (n h) -> p n h", n=3), AX_X, ALU.add))
                    link(v.tensor_scalar(nw[:, 0, :], nw[:, 0, :], TINY, None, ALU.max))
                    rsqrt(nw[:, 1, :], nw[:, 0, :], nw[:, 2, :], nw[:, 3, :].bitcast(I32))
                    link(v.tensor_scalar(fac3[:], nw[:, 1, N:N + 3], RHO * RADIUS, RHO, ALU.mult, ALU.min))
                    link(v.scalar_tensor_tensor(fac[:], nw[:, 1, 0:N].rearrange("p (n h) -> p n h", n=3), RADIUS,
                                                fac3[:].rearrange("p (n o) -> p n o", o=1).broadcast_to([P, 3, H]),
                                                ALU.mult, ALU.min))
                    link(v.tensor_scalar(fac[:, 0, :], fac[:, 0, :], 1.0 / math.sqrt(HD), None, ALU.mult))

                    def head(ap, n, r0=0, r1=P):
                        return (ap[r0:r1, n * D:(n + 1) * D].rearrange("p (h d) -> p h d", h=H),
                                fac[r0:r1, n, :].rearrange("p (h o) -> p h o", o=1).broadcast_to([r1 - r0, H, HD]))
                    yk, fk = head(y, 1)
                    dve.wait_ge(s["k1_a"], 2 * m + e)
                    v.tensor_tensor(kf[:].rearrange("p (h d) -> p h d", h=H), yk, fk, ALU.mult).then_inc(s["f_v"], 1)
                    yq, fq = head(y, 0)
                    v.tensor_tensor(qf[:, bass.ds(2 * m + e, 1), :].rearrange("p a (h d) -> p (a h) d", h=H), yq, fq, ALU.mult)
                    for b in range(B):
                        yv, fv = head(y, 2, b * TOK, (b + 1) * TOK)
                        v.tensor_tensor(vals[e * TOK:(e + 1) * TOK, bass.ds(m, 1), b, :, 0:HD]
                                        .rearrange("p a h d -> p (a h) d"),
                                        yv, fv, ALU.mult).then_inc(s["v_v"], 1)
                    dve.wait_ge(s["k1_a"], n1)
                    v.tensor_tensor(resid[:].rearrange("p (h d) -> p h d", h=H), kf[:].rearrange("p (h d) -> p h d", h=H),
                                    stackb[:, :, 0, :], ALU.subtract).then_inc(s["r1_v"], 1)
                    dve.wait_ge(s["k2_a"], n1)
                    v.tensor_tensor(stackb[:, :, 5, :], resid[:].rearrange("p (h d) -> p h d", h=H),
                                    stackb[:, :, 3, :], ALU.subtract).then_inc(s["k3_v"], 1)
                    dve.wait_ge(s["kst_pe"], 4 * m + 2 * e + 2)
                    v.tensor_copy(kT[:, 8:16, :, bass.ds((2 * m + e) * TOK, TOK)],
                                  bank[4][:].bitcast(BF16)[0:96, :].rearrange("p (h b t) -> p h b t", h=8, b=B))\
                        .then_inc(s["kev_v"], 1)

            def att(i):
                i1 = i + 1
                dve.wait_ge(s["q1_a"], i1)
                r = resid[:].rearrange("p (h d) -> p h d", h=H)
                v.tensor_tensor(r, qf[:, bass.ds(i, 1), :].rearrange("p a (h d) -> p (a h) d", h=H),
                                stackb[:, :, 0, :], ALU.subtract).then_inc(s["qr_v"], 1)
                dve.wait_ge(s["q2_a"], i1)
                v.tensor_tensor(stackb[:, :, 2, :], r, stackb[:, :, 1, :], ALU.subtract).then_inc(s["q3_v"], 1)
                dve.wait_ge(s["qst_pe"], 2 * i + 2)
                dve.wait_ge(s["s_pe"], 32 * i)
                v.tensor_copy(qT[:, 8:16, :], bank[4][:].bitcast(BF16)[0:96, :].rearrange("p (h t) -> p h t", h=8))\
                    .then_inc(s["qev_v"], 1)

            def post(i):
                i1 = i + 1
                restart()
                to = s_bank[0][:].rearrange("p (h r) -> p h r", h=H)
                dve.wait_ge(s["to_pe"], i1)
                dve.wait_ge(s["osq_a"], i1)
                link(v.reciprocal(fac[:, 0, :], to[:, :, HD]))
                link(v.tensor_reduce(fac[:, 1, :], junk_a[:, 0:D].rearrange("p (h d) -> p h d", h=H), AX_X, ALU.add))
                link(v.tensor_tensor(nw[:, 0, 0:H], fac[:, 1, :], fac[:, 0, :], ALU.mult))
                link(v.tensor_tensor(nw[:, 0, 0:H], nw[:, 0, 0:H], fac[:, 0, :], ALU.mult))
                link(v.tensor_scalar(nw[:, 0, 0:H], nw[:, 0, 0:H], TINY, None, ALU.max))
                rsqrt(nw[:, 1, 0:H], nw[:, 0, 0:H], nw[:, 2, 0:H], nw[:, 3, 0:H].bitcast(I32))
                link(v.tensor_scalar(nw[:, 1, 0:H], nw[:, 1, 0:H], RADIUS / RHO, 1.0 / RHO, ALU.mult, ALU.min))
                link(v.tensor_tensor(nw[:, 2, 0:H], nw[:, 1, 0:H], nw[:, 1, 0:H], ALU.mult))
                link(v.tensor_tensor(nw[:, 2, 0:H], nw[:, 2, 0:H], nw[:, 0, 0:H], ALU.mult))
                v.tensor_reduce(scal[:, 31, 0:1], nw[:, 2, 0:H], AX_X, ALU.add).then_inc(s["of_v"], 1)
                link(v.tensor_tensor(nw[:, 1, 0:H], nw[:, 1, 0:H], fac[:, 0, :], ALU.mult))
                v.tensor_tensor(wa[:].rearrange("p (h d) -> p h d", h=H), to[:, :, 0:HD],
                                nw[:, 1, 0:H].rearrange("p (h o) -> p h o", o=1).broadcast_to([P, H, HD]),
                                ALU.mult).then_inc(s["zt_v"], 1)
                dve.wait_ge(s["wo_pe"], i1)
                dve.wait_ge(s["oss_g"], i1)
                v.scalar_tensor_tensor(wa[:], m_bank[:, 256:512], scal[:, 31, 1:2], bo[:], ALU.mult, ALU.add)\
                    .then_inc(s["yo_v"], 1)
                dve.wait_ge(s["co_g"], i1)
                v.scalar_tensor_tensor(wb[:], wa[:], scal[:, 32, 1:2], mod[:, 2 * D:3 * D], ALU.mult, ALU.mult)\
                    .then_inc(s["w_v"], 1)
                dve.wait_ge(s["w_v"], i1)
                dve.wait_ge(s["xin_in"], 32 * i + 32)
                v.tensor_tensor_reduce(junk_v[:], wb[:], xin[:], 1.0, 0.0, ALU.mult, ALU.add, scal[:, 33, 1:2])\
                    .then_inc(s["wx_v"], 1)
                dve.wait_ge(s["mob_g"], i1)
                link(v.tensor_scalar(wb[:], wb[:], scal[:, 34, 1:2], None, ALU.mult))
                link(v.scalar_tensor_tensor(x1[:], xin[:], scal[:, 34, 0:1], wb[:], ALU.mult, ALU.add))
                link(v.bn_stats(bns[:], x1[:]))
                v.bn_aggr(scal[:, 35, 0:2], bns[:]).then_inc(s["bn_v"], 1)
                dve.wait_ge(s["th_g"], i1)
                guess(1).then_inc(s["th_a"], 1)
                dve.wait_ge(s["th2_a"], i1)
                correct(1).then_inc(s["th3_g"], 1)
                dve.wait_ge(s["xn2_a"], i1)
                link(v.tensor_tensor(wb[:], wa[:], mod[:, 4 * D:5 * D], ALU.mult))
                v.tensor_tensor(wb[:], wb[:], mod[:, 3 * D:4 * D], ALU.add).then_inc(s["t2_v"], 1)
                dve.wait_ge(s["c2_g"], i1)
                dve.wait_ge(s["f1_pe"], i1)
                v.scalar_tensor_tensor(y1[:, 0:512], s_bank[0][:, :], scal[:, 37, 1:2], bf1[:, 0:512], ALU.mult, ALU.add)
                v.scalar_tensor_tensor(y1[:, 512:1024], s_bank[1][:, :], scal[:, 37, 1:2], bf1[:, 512:1024],
                                       ALU.mult, ALU.add).then_inc(s["y1_v"], 1)
                dve.wait_ge(s["c3_g"], i1)
                dve.wait_ge(s["f2_pe"], i1)
                v.scalar_tensor_tensor(wa[:], m_bank[:, 256:512], scal[:, 38, 1:2], bf2[:], ALU.mult, ALU.add)\
                    .then_inc(s["y2_v"], 1)
                dve.wait_ge(s["c4_g"], i1)
                v.scalar_tensor_tensor(wb[:], wa[:], scal[:, 39, 1:2], mod[:, 5 * D:6 * D], ALU.mult, ALU.mult)\
                    .then_inc(s["w2_v"], 1)
                dve.wait_ge(s["w2_v"], i1)
                v.tensor_tensor_reduce(junk_v[:], wb[:], x1[:], 1.0, 0.0, ALU.mult, ALU.add, scal[:, 33, 4:5])\
                    .then_inc(s["w2x_v"], 1)
                dve.wait_ge(s["mob2_g"], i1)
                link(v.tensor_scalar(wb[:], wb[:], scal[:, 34, 3:4], None, ALU.mult))
                link(v.scalar_tensor_tensor(wb[:], x1[:], scal[:, 34, 2:3], wb[:], ALU.mult, ALU.add))
                v.tensor_tensor(xo[:], wb[:], xin[:], ALU.add).then_inc(s["xo_v"], 1)

            def rnn_step(i, t):
                z = z_bank[(t // BLK) % 2]
                dve.wait_ge(s["z_pe_step"], i * TOK + t + 1)
                v.transpose(z[:, 64:128], z[:, 0:64]).then_inc(s["tr_v"], 1)

            def store(i):
                dve.wait_ge(s["flush_pe"], i + 1)
                dve.wait_ge(s["out_dma"], 32 * i)
                v.tensor_tensor(oat[:], m_bank[:, 0:256], xo[:], ALU.add).then_inc(s["out_v"], 1)

            with dve.Fori(0, TILES) as i:
                att(i)
                post(i)
                for t in range(TOK):
                    rnn_step(i, t)
                store(i)

        @block.tensor
        def _(pe):
            t_ = nc.tensor
            pe.wait_ge(s["cond_spread"], 13)
            pe.wait_ge(s["cond_in"], 80)
            pe.wait_ge(s["gconst"], 5)
            for n in range(3):
                for c in range(DC):
                    t_.matmul(bank[n][:, :], cond_rows[:, c, :], wada_sb[:, c, n * 512:(n + 1) * 512],
                              start=(c == 0), stop=False)
                mm = t_.matmul(bank[n][:, :], ones_row[:], bada_row[:, n * 512:(n + 1) * 512], start=False, stop=True)
            mm.then_inc(s["ada_done"], 1)
            pe.wait_ge(s["mod_done"], 5)
            pe.wait_ge(s["w_in"], 16 * 11)

            def turn(dst, src, chunks):
                for c in range(chunks):
                    mm = t_.transpose(dst[:, c * P:(c + 1) * P], src[:, c * P:(c + 1) * P], ident[:])
                return mm

            def stack_turn(half):
                dst = bank[3 + half][:].bitcast(BF16)
                for h in range(8):
                    mm = t_.transpose(dst[0:96, h * P:(h + 1) * P],
                                      stackb[:, 8 * half + h, :, :].rearrange("p a d -> p (a d)"), ident_bf[:])
                return mm

            with pe.Fori(0, TILES // 2) as m:
                for e in range(2):
                    n1 = 2 * m + e + 1
                    pe.wait_ge(s["t1_v"], n1)
                    if e == 0:
                        pe.wait_ge(s["t1T_a"], 2 * m)
                    else:
                        pe.wait_ge(s["t1T_a"], 2 * m + 1)
                    turn(bank[0][:, e * D:(e + 1) * D], t1[:, e, :], DC).then_inc(s["t1_pe"], 1)
                    pe.wait_ge(s["t1T_a"], n1)
                    pe.wait_ge(s["y_v"], 2 * m + e)
                    for c in range(DC):
                        t_.matmul(bank[1][:, :], t1T[:, e, c, :], wqkv[:, c, 0:512], start=(c == 0), stop=(c == DC - 1))
                    for c in range(DC):
                        mm = t_.matmul(bank[2][:, 0:D], t1T[:, e, c, :], wqkv[:, c, 512:768],
                                       start=(c == 0), stop=(c == DC - 1))
                    mm.then_inc(s["qkv_pe"], 1)
                    pe.wait_ge(s["k3_v"], n1)
                    pe.wait_ge(s["kev_a"], 2 * m + e)
                    stack_turn(0).then_inc(s["kst_pe"], 1)
                    pe.wait_ge(s["kev_v"], 2 * m + e)
                    stack_turn(1).then_inc(s["kst_pe"], 1)

            def att(i):
                i1 = i + 1
                pe.wait_ge(s["kev_a"], TILES)
                pe.wait_ge(s["kev_v"], TILES)
                pe.wait_ge(s["v_v"], 2 * TILES)
                pe.wait_ge(s["xT_a"], i)
                pe.wait_ge(s["q3_v"], i1)
                stack_turn(0).then_inc(s["qst_pe"], 1)
                stack_turn(1).then_inc(s["qst_pe"], 1)
                pe.wait_ge(s["qev_a"], i1)
                pe.wait_ge(s["qev_v"], i1)
                for u in range(32 + 4):
                    if u < 32:
                        g, b, j = u // 8, (u // 4) % 2, u % 4
                        h = QUAD * g + j
                        if u >= 4:
                            pe.wait_ge(s["p_a"], 32 * i + u - 3)
                        for k in range(KC):
                            mm = t_.matmul(s_bank[u % 4][:, k * TOK:(k + 1) * TOK], kT[:, h, b, k * P:(k + 1) * P],
                                           qT[:, h, b * TOK:(b + 1) * TOK], start=(k == 0), stop=(k == KC - 1),
                                           skip_group_check=True)
                        mm.then_inc(s["s_pe"], 1)
                    if u >= 4 and u % 4 == 3:
                        w = u // 4 - 1
                        g, b = w // 2, w % 2
                        pe.wait_ge(s["p_a"], 32 * i + 4 * w + 4)
                        for k in range(KC):
                            for j in range(QUAD):
                                mm = t_.matmul(o_bank[32 * j:32 * j + HD + 1, w * TOK:(w + 1) * TOK],
                                               vals[:, k, b, QUAD * g + j, :], probs[:, w % 2, j, k * TOK:(k + 1) * TOK],
                                               start=(k == 0), stop=(k == KC - 1), skip_group_check=True)
                        mm.then_inc(s["pv_pe"], 1)

            def post(i):
                i1 = i + 1
                pe.wait_ge(s["o_ev"], i1)
                turn(s_bank[0], oT, 4).then_inc(s["to_pe"], 1)
                pe.wait_ge(s["zt_v"], i1)
                turn(m_bank, wa, DC).then_inc(s["z_pe"], 1)
                pe.wait_ge(s["zc_a"], i1)
                for c in range(DC):
                    mm = t_.matmul(m_bank[:, 256:512], aT[:, c, :], wo[:, c, :], start=(c == 0), stop=(c == DC - 1))
                mm.then_inc(s["wo_pe"], 1)
                pe.wait_ge(s["t2_v"], i1)
                turn(m_bank, wb, DC).then_inc(s["t2_pe"], 1)
                pe.wait_ge(s["t2T_a"], i1)
                for n in range(2):
                    for c in range(DC):
                        mm = t_.matmul(s_bank[n][:, :], aT[:, c, :], wf1[:, c, n * 512:(n + 1) * 512],
                                       start=(c == 0), stop=(c == DC - 1))
                mm.then_inc(s["f1_pe"], 1)
                pe.wait_ge(s["y1_v"], i1)
                turn(s_bank[2], y1[:, 0:512], 4).then_inc(s["y1_pe"], 1)
                turn(s_bank[3], y1[:, 512:1024], 4).then_inc(s["y1_pe"], 1)
                pe.wait_ge(s["y1T_a"], i1)
                for c in range(FC):
                    mm = t_.matmul(m_bank[:, 256:512], y1T[:, c, :], wf2[:, c, :], start=(c == 0), stop=(c == FC - 1))
                mm.then_inc(s["f2_pe"], 1)
                pe.wait_ge(s["xo_v"], i1)
                turn(m_bank, xo, DC).then_inc(s["xo_pe"], 1)

            def inputs(i, k):
                z = z_bank[k % 2]
                for c in range(DC):
                    xs = xT[:, c, B * BLK * k:B * BLK * (k + 1)]
                    for j in range(QUAD):
                        t_.matmul(z[32 * j:32 * j + 32, 0:64], xs, wx[:, c, 64 * j:64 * j + 64],
                                  start=(c == 0), stop=False, skip_group_check=True)
                for j in range(QUAD):
                    t_.matmul(z[32 * j:32 * j + 32, 0:64], ones_row[:, 0:32], bh_row[:, 64 * j:64 * j + 64],
                              start=False, stop=False, skip_group_check=True)

            def rnn_step(i, t):
                m = t % BLK
                z = z_bank[(t // BLK) % 2]
                base = 32 * (t if t else TOK) - 2 * m
                if t or i is not None:
                    pe.wait_ge(s["h_a"], i * TOK + t)
                for c in range(2):
                    for j in range(QUAD):
                        mm = t_.matmul(z[32 * j:32 * j + 32, 0:64], hist[:, c, base:base + 32],
                                       wh[:, c, 64 * j:64 * j + 64], start=False, stop=(c == 1 and m == BLK - 1),
                                       skip_group_check=True)
                mm.then_inc(s["z_pe_step"], 1)

            def flush(i):
                for hh in range(2):
                    for c in range(2):
                        for b in range(B):
                            o = 32 * (32 * hh + 1)
                            hs = hist[:, c, o:o + 32 * 32].rearrange("p (s r) -> p s r", r=32)[:, :, b]
                            q = b * TOK + 32 * hh
                            mm = t_.matmul(m_bank[q:q + 32, 0:256], hs, perm[:, c, :], start=(c == 0), stop=(c == 1),
                                           skip_group_check=True)
                return mm

            with pe.Fori(0, TILES) as i:
                att(i)
                post(i)
                pe.wait_ge(s["xT_a"], i + 1)
                pe.wait_ge(s["h0_in"], 16 * 8)
                inputs(i, 0)
                for t in range(TOK):
                    rnn_step(i, t)
                    if t % BLK == 4 and t // BLK + 1 < TOK // BLK:
                        inputs(i, t // BLK + 1)
                pe.wait_ge(s["h_a"], i * TOK + TOK)
                flush(i).then_inc(s["flush_pe"], 1)


_INS = ['x', 'cond_1024', 'L0_cond_w_q', 'L0_cond_b_q', 'L0_cond_w_k', 'L0_cond_b_k', 'L0_cond_w_v', 'L0_cond_b_v',
        'L0_cond_w_o', 'L0_cond_b_o', 'L0_cond_w_f1', 'L0_cond_b_f1', 'L0_cond_w_f2', 'L0_cond_b_f2',
        'L0_cond_w_ada', 'L0_cond_b_ada', 'L1_cond_Wx', 'L1_cond_Wh', 'L1_cond_b']


def kernel(**inputs):
    import numpy as _np
    import concourse.bacc as _bacc
    from concourse import mybir as _mybir
    from concourse.bass_utils import run_bass_kernel_spmd as _run

    nc = _bacc.Bacc("TRN2", target_bir_lowering=False, num_devices=1)
    arrays, args = {}, []
    for name in _INS:
        a = _np.ascontiguousarray(inputs[name])
        arrays[f"in_{name}_dram"] = a
        args.append(nc.dram_tensor(f"in_{name}_dram", a.shape, _mybir.dt.from_np(a.dtype), kind="ExternalInput").ap())
    args.append(nc.dram_tensor("out_0_dram", (2, 1024, 256), _mybir.dt.float32, kind="ExternalOutput").ap())
    build(nc, *args)
    r = _run(nc, [arrays], core_ids=[0])
    return r.results[0]["out_0_dram"]
```

```python
import math
from contextlib import ExitStack

import numpy as np

import concourse.bass as bass
from concourse import mybir

F32 = mybir.dt.float32
BF16 = mybir.dt.bfloat16
I32 = mybir.dt.int32
ALU = mybir.AluOpType
ACT = mybir.ActivationFunctionType
AX_X = mybir.AxisListType.X

P = 128
B, S, D = 2, 1024, 256
H, HD, FF = 16, 16, 1024
TOK = P // B
TILES = S // TOK
DC = D // P
FC = FF // P
KC = S // P
PARTS = 6
QUAD = 4
HG = H // QUAD
BLK = 8
ROWS = B * BLK
HALF = TOK // 2

LEAD = 11
LOOP = (1, TILES - 3)


def live(tile):
    return not isinstance(tile, int) or 0 <= tile < TILES


def wait(eng, semaphore, value):
    if not isinstance(value, int) or value > 0:
        eng.wait_ge(semaphore, value)


def walk(eng, slot):
    for n in range(-3, LOOP[0]):
        for t in range(TOK):
            slot(n, t)
    with eng.Fori(*LOOP) as n:
        for t in range(TOK):
            slot(n, t)
    for n in range(LOOP[1], TILES + 1):
        for t in range(TOK):
            slot(n, t)


def parts(n, t, att, post):
    if t < TOK - LEAD and live(n + 2):
        att(n + 2, t + LEAD)
    if t >= TOK - LEAD + Q1 and live(n + 3):
        att(n + 3, t + LEAD - TOK)
    if live(n + 1):
        post(n + 1, t + LEAD)
    if t >= TOK - LEAD and live(n + 2):
        post(n + 2, t + LEAD - TOK)


Q1, Q2, Q3, QT, QE = -11, -9, -8, -6, -4
SCORES, EXP_LAG = -2, 1
O_COPY, O_TURN, O_SQUARE, HEADS, Z_TURN, Z_COPY, WO, YO = 0, 1, 3, 4, 11, 12, 13, 15
GATE, MOB_TANH, X1, LOG_GUESS, LOG_TANH, LOG_FIX, NORM, T2 = 17, 20, 25, 29, 30, 31, 37, 38
T2_TURN, F1, Y1A, Y1B, Y1_TURN, Y1_COPY = 39, 41, 45, 49, (46, 50), (48, 52)
F2, Y2, GATE2, MOB2_TANH, XO, XO_TURN = 49, 57, 59, 62, 67, 70
BIAS = 1
INPUTS = 2
FIRST_INPUTS = 61
FLUSH = (49, 5)
HOLD = 12


def fixed_costs():
    cost = [0.0] * TOK
    for L, c in ((QT, 2), (Z_TURN, 1), (WO, DC), (T2_TURN, 1), (XO_TURN, 1), (O_TURN, 2), (F1, FC), (F2, FC),
                 (Y1_TURN[0], 2), (Y1_TURN[1], 2)):
        for n in range(c):
            cost[(L + n) % TOK] += 2
    for c in range(2):
        for at in FLUSH:
            cost[(LEAD + at + c) % TOK] += 2.5
        cost[(LEAD + FIRST_INPUTS + c) % TOK] += 1
        for k in range(TOK // BLK - 1):
            cost[(LEAD + BLK * k + INPUTS + c) % TOK] += 1
    return cost


def plan(unit_limit, chunk_limit):
    cost, scores, outputs = fixed_costs(), {}, {}
    units, chunks = {}, {}
    for at in range(SCORES, TOK):
        load, scores[at], outputs[at] = cost[at % TOK], [], []
        u = len(units)
        free = u < 2 or units[u - 2] + EXP_LAG < at
        free = free and (u < 8 or KC * (u // 4 - 1) - 1 in chunks)
        if u < H * B and free and load + 2.1 <= unit_limit:
            units[u] = at
            scores[at].append(u)
            load += 2.1
        while len(chunks) < H // QUAD * B * KC and load + 0.9 <= chunk_limit:
            k = len(chunks)
            last = 4 * (k // KC) + 3
            if last not in units or units[last] + EXP_LAG >= at:
                break
            chunks[k] = at
            outputs[at].append(k)
            load += 0.9
        cost[at % TOK] = load
    assert len(chunks) == H // QUAD * B * KC
    return scores, outputs, cost


SCORE_UNITS, OUTPUT_CHUNKS, LOAD = plan(4.2, 3.7)
FILL = 2
CLOCK_LOAD = 2.5

EPS = 1e-7
MAXN = float(np.float32(1.0 - 1e-05))
RADIUS = math.atanh(MAXN)
TINY = 1e-30


def _beta(a, b):
    return math.exp(math.lgamma(a) + math.lgamma(b) - math.lgamma(a + b))


BETA_N = _beta(D / 2, 0.5)
BETA_H = _beta(HD / 2, 0.5)
RHO = BETA_H / BETA_N
ONE_BITS = float(127 << 23)
LOG_STEP = 0.5 * math.log(2.0) * 2.0 ** -23
MAGIC = float(0x5F3759DF)


def build(nc, x, cond, w_q, b_q, w_k, b_k, w_v, b_v, w_o, b_o, w_f1, b_f1, w_f2, b_f2, w_ada, b_ada,
          w_x, w_h, b_h, out):
    with ExitStack() as ctx:
        def sb(name, shape, dt=F32):
            return ctx.enter_context(nc.sbuf_tensor(name, shape, dt))

        def sem(name):
            return ctx.enter_context(nc.semaphore(name))

        kT = sb("kT", [96, H, B, S], BF16)
        vals = sb("vals", [P, KC, B, H, HD + 1])
        xp_buf = sb("xp_buf", [P, TILES * D])
        x_all = xp_buf[:].rearrange("p (i d) -> p i d", d=D)
        probs = xp_buf[:].rearrange("p (g j n) -> p g j n", g=2, j=QUAD)
        qf = sb("qf", [P, TILES, D])
        wada_sb = qf[:].rearrange("p i d -> p (i d)")[:, 0:DC * 6 * D].rearrange("p (c n) -> p c n", c=DC)
        wo = sb("wo", [P, DC, D])
        wf1 = sb("wf1", [P, DC, FF])
        wf2 = sb("wf2", [P, FC, D])
        wx = sb("wx", [P, DC, D])
        wh = sb("wh", [P, 2, D])
        perm = sb("perm", [P, 2, D])
        bh = sb("bh", [P, D // QUAD])
        mod = sb("mod", [P, 6 * D])
        bo = sb("bo", [P, D])
        bf1 = sb("bf1", [P, FF])
        bf2 = sb("bf2", [P, D])
        bada_row = kT[0:1].rearrange("p h b s -> p (h b s)").bitcast(F32)[:, 0:6 * D]
        condT = sb("condT", [P, DC, B])
        cond_rows = sb("cond_rows", [P, DC, P])
        ident = sb("ident", [P, P])
        ident_bf = sb("ident_bf", [P, P], BF16)
        tiny = sb("tiny", [P, 1])
        ones_row = sb("ones_row", [1, P])
        halves = sb("halves", [P, 2, TILES])
        hist = sb("hist", [P, 2, (TOK + 1) * ROWS])
        xT = sb("xT", [P, DC, P])
        scal = sb("scal", [P, 40, TILES])
        alpha_all = sb("alpha_all", [P, TILES])
        beta_all = sb("beta_all", [P, TILES])
        resid = sb("resid", [P, D])
        work = sb("work", [P, 24 * D])

        def carve(*sizes):
            at, parts = 0, []
            for n in sizes:
                parts.append(work[:, at:at + n])
                at += n
            return parts

        wqkv, t1, t1T, y, ysq, kf, junk_p, bqkv = carve(DC * 3 * D, 2 * D, 2 * D, 3 * D, 3 * D, D, 2 * D, 3 * D)
        wqkv = wqkv.rearrange("p (c n) -> p c n", c=DC)
        t1 = t1.rearrange("p (e d) -> p e d", e=2)
        t1T = t1T.rearrange("p (e c t) -> p e c t", e=2, c=DC)
        oT, y1, y1T, junk_a, xin, wa, wb, junk_v, x1, xo, aT, oat, wc, xhold = carve(2 * D, FF, FF, FF, D, D, D, D, D, D, D, D, D, D)
        y1T = y1T.rearrange("p (c t) -> p c t", c=FC)
        aT = aT.rearrange("p (c t) -> p c t", c=DC)
        stackb = sb("stackb", [P, H, PARTS, HD], BF16)
        qT = sb("qT", [96, H, P], BF16)
        nw = sb("nw", [P, 4, 3 * H + 3])
        fac = sb("fac", [P, 3, H])
        fac3 = sb("fac3", [P, 3])
        c1 = sb("c1", [P, 2])
        ss1 = sb("ss1", [P, 2])
        c1t = sb("c1t", [P, 2])
        bns = sb("bns", [P, 6])
        bna = sb("bna", [P, TILES, 2])

        bank = [ctx.enter_context(nc.psum_tensor(f"bank{n}", [P, 512], F32)) for n in range(8)]
        z_bank = bank[0:2]
        s_bank = bank[2:4]
        a_bank, b_bank = bank[4:6]
        o_bank = bank[6]
        m_bank = bank[7]

        names = """x_in w_in b_in cond_in gconst gmem ada_done cond_spread mod_done
            st_v st_g st_a st_n xn_a t1_v ss_a c1_g t1_pe t1T_a qkv_pe y_v sq_a f_v
            k1_a r1_v k2_a k3_v kst_pe kev_a kev_v v_v h0_in
            qr_v q1_a q2_a q3_v qst_pe qev_a qev_v s_pe p_a pv_pe
            o_ev to_pe osq_a of_v zt_v oss_g z_pe zc_a wo_pe yo_v yo2_a co_g w_v w2_a wx_v mob_g x1_v bn_v
            th_a th_g th2_a th3_g ln_g xn2_a t2_v t2s_a c2_g t2_pe t2T_a f1_pe y1_v y1s_a c3_g y1_pe y1T_a f2_pe
            y2_v y2s_a c4_g w2_v w22_a w2x_v tm_g tm_a mob2_g xo_v xo_pe xT_a xin_in x_held h0_a y1sb_a
            bias_v bits_pe z_pe_step tr_v h_a flush_pe out_v out_dma""".split()
        s = {n: sem(n) for n in names}
        dve_link, pool_link, act_link = sem("dve_link"), sem("pool_link"), sem("act_link")
        block = ctx.enter_context(nc.Block())

        def chain(eng, link_sem):
            count = [0]

            def link(ins):
                count[0] += 1
                ins.then_inc(link_sem, 1)
                eng.wait_ge(link_sem, count[0])

            def then(ins):
                count[0] += 1
                ins.then_inc(link_sem, 1)

            def last():
                if count[0]:
                    eng.wait_ge(link_sem, count[0])

            def restart():
                last()
                eng.sem_clear(link_sem)
                count[0] = 0
            return link, then, last, restart

        def rows_of(v):
            return v.rearrange("(a n) -> a n", a=1)

        @block.sync
        def _(sp):
            for b in range(B):
                for h in range(2):
                    src = x[b].rearrange("(i t) d -> t i d", t=TOK)
                    sp.dma_start(x_all[b * TOK:(b + 1) * TOK, 8 * h:8 * h + 8, :],
                                 src[:, 8 * h:8 * h + 8, :]).then_inc(s["x_in"], 16)
            for n, w in enumerate((w_q, w_k, w_v)):
                sp.dma_start(wqkv[:, :, n * D:(n + 1) * D],
                             w.rearrange("(c p) n -> p c n", p=P)).then_inc(s["w_in"], 16)
            for dst, w in ((wo, w_o), (wf1, w_f1), (wf2, w_f2), (wx, w_x)):
                sp.dma_start(dst[:], w.rearrange("(c p) n -> p c n", p=P)).then_inc(s["w_in"], 16)
            whv = w_h.rearrange("(j c p) n -> j p c n", c=2, p=32)
            for j in range(QUAD):
                sp.dma_start(wh[32 * j:32 * j + 32, :, :], whv[j]).then_inc(s["w_in"], 16)

            def slot(n, t):
                if t == 0 and live(n + 1):
                    wait(sp, s["xo_v"], n + 1)
                    if isinstance(n, int) and n == -1:
                        sp.wait_ge(s["kev_v"], TILES)
                    for b in range(B):
                        sp.dma_start(xin[b * TOK:(b + 1) * TOK, :],
                                     x[b, bass.ds((n + 1) * TOK, TOK), :]).then_inc(s["xin_in"], 16)
                if t == HOLD and live(n):
                    wait(sp, s["out_v"], 2 * n)
                    sp.wait_ge(s["xo_v"], n + 1)
                    sp.dma_start(xhold[:], xo[:]).then_inc(s["x_held"], 16)
                for hh, at in ((1, 9), (0, 53)):
                    m = n - hh
                    if t == at and (not isinstance(n, int) or 0 <= m < TILES):
                        sp.wait_ge(s["out_v"], 2 * m + hh + 1)
                        for b in range(B):
                            q = b * TOK + HALF * hh
                            sp.dma_start(out[b, bass.ds(m * TOK + HALF * hh, HALF), :],
                                         oat[q:q + HALF, :]).then_inc(s["out_dma"], 16)

            walk(sp, slot)
            sp.wait_ge(s["out_dma"], 2 * B * 16 * TILES)

        @block.gpsimd
        def _(pool):
            g = nc.gpsimd
            link, then, last, restart = chain(pool, pool_link)
            g.memset(tiny[:], TINY).then_inc(s["gconst"], 1)
            g.memset(ones_row[:], 1.0).then_inc(s["gconst"], 1)
            g.memset(halves[:, 0, :], 0.5).then_inc(s["gconst"], 1)
            g.memset(halves[:, 1, :], -0.5).then_inc(s["gconst"], 1)
            link(g.memset(ident[:], 0.0))
            g.affine_select(out=ident[:], in_=ident[:], compare_op=ALU.not_equal, fill=1.0, base=0,
                            pattern=[[-1, P]], channel_multiplier=1).then_inc(s["gconst"], 1)
            g.memset(perm[:], 0.0).then_inc(s["gmem"], 1)
            g.memset(vals[:], 1.0).then_inc(s["gmem"], 1)
            g.memset(hist[:], 0.0).then_inc(s["gmem"], 1)
            pool.wait_ge(s["gconst"], 5)

            def power(dst, src, half, n):
                link(g.tensor_tensor(dst, src, halves[:, half, 0:n], ALU.pow))

            def sc(k, n=1):
                return scal[:, k, 0:n]

            def log_a(mean, var, n):
                link(g.tensor_tensor(sc(0, n), mean, mean, ALU.mult))
                link(g.tensor_tensor(sc(0, n), sc(0, n), var, ALU.add))
                link(g.tensor_scalar(sc(1, n), sc(0, n), float(D), 0.0, ALU.mult, ALU.max))
                power(sc(2, n), sc(1, n), 0, n)
                link(g.tensor_scalar(sc(2, n), sc(2, n), EPS, None, ALU.max))
                link(g.tensor_scalar(sc(3, n), sc(2, n), MAXN, None, ALU.min))

            def log_b(mean, var, alpha, beta, n):
                link(g.tensor_tensor(sc(9, n), sc(8, n), sc(8, n), ALU.mult))
                link(g.tensor_scalar(sc(10, n), sc(9, n), 0.2, 1.0 / 3.0, ALU.mult, ALU.add))
                link(g.tensor_tensor(sc(10, n), sc(10, n), sc(9, n), ALU.mult))
                link(g.tensor_scalar(sc(10, n), sc(10, n), 1.0, 1.0, ALU.mult, ALU.add))
                link(g.tensor_tensor(sc(10, n), sc(10, n), sc(8, n), ALU.mult))
                link(g.tensor_tensor(sc(10, n), sc(10, n), sc(5, n), ALU.add))
                link(g.tensor_tensor(sc(11, n), sc(10, n), sc(13, n), ALU.mult))
                link(g.tensor_tensor(sc(12, n), sc(11, n), sc(11, n), ALU.mult))
                link(g.tensor_tensor(sc(12, n), sc(12, n), var, ALU.mult))
                link(g.tensor_scalar(sc(12, n), sc(12, n), 1e-6, 0.0, ALU.add, ALU.max))
                power(sc(14, n), sc(12, n), 1, n)
                link(g.tensor_tensor(alpha, sc(14, n), sc(11, n), ALU.mult))
                link(g.tensor_tensor(sc(15, n), alpha, mean, ALU.mult))
                return g.tensor_scalar(beta, sc(15, n), -1.0, 0.0, ALU.mult, ALU.add)

            def clip(dst, src, tmp, factor=RADIUS):
                link(g.tensor_tensor(tmp, src, tiny[:], ALU.add))
                power(tmp, tmp, 1, 1)
                return g.tensor_scalar(dst, tmp, factor, 1.0, ALU.mult, ALU.min)

            pool.wait_ge(s["st_v"], 1)
            log_a(bna[:, :, 0], bna[:, :, 1], TILES)
            g.tensor_copy(sc(16, TILES), sc(3, TILES)).then_inc(s["st_g"], 1)
            pool.wait_ge(s["st_n"], 2)
            log_b(bna[:, :, 0], bna[:, :, 1], alpha_all[:], beta_all[:], TILES).then_inc(s["st_g"], 1)

            restart()
            with pool.Fori(0, TILES // 2) as m:
                for e in range(2):
                    pool.wait_ge(s["ss_a"], 2 * m + e + 1)
                    clip(c1[:, e:e + 1], ss1[:, e:e + 1], c1t[:, e:e + 1]).then_inc(s["c1_g"], 1)
                restart()

            def mobius(n_tanh, ss_w, dot, ss_x, p_out, q_out, tm_g, tm_a, i1):
                power(sc(20), ss_w, 0, 1)
                link(g.tensor_scalar(sc(20), sc(20), EPS, None, ALU.max))
                power(sc(22), sc(20), 1, 1)
                g.tensor_tensor(sc(22), sc(22), sc(22), ALU.mult).then_inc(tm_g, 1)
                pool.wait_ge(tm_a, i1)
                link(g.tensor_tensor(sc(23), sc(21), sc(22), ALU.mult))
                link(g.tensor_tensor(sc(24), sc(23), sc(23), ALU.mult))
                link(g.tensor_tensor(sc(24), sc(24), ss_w, ALU.mult))
                link(g.tensor_tensor(sc(25), sc(23), dot, ALU.mult))
                link(g.tensor_scalar(sc(26), sc(25), 2.0, 1.0, ALU.mult, ALU.add))
                link(g.tensor_tensor(sc(27), sc(26), sc(24), ALU.add))
                link(g.tensor_tensor(sc(28), ss_x, sc(24), ALU.mult))
                link(g.tensor_tensor(sc(28), sc(28), sc(26), ALU.add))
                link(g.tensor_scalar(sc(28), sc(28), EPS, None, ALU.max))
                power(sc(29), sc(28), 1, 1)
                link(g.tensor_tensor(sc(29), sc(29), sc(29), ALU.mult))
                link(g.tensor_tensor(p_out, sc(27), sc(29), ALU.mult))
                link(g.tensor_scalar(sc(30), ss_x, -1.0, 1.0, ALU.mult, ALU.add))
                link(g.tensor_tensor(sc(30), sc(30), sc(29), ALU.mult))
                return g.tensor_tensor(q_out, sc(30), sc(23), ALU.mult)

            def post(i, L):
                i1 = i + 1
                if L == HEADS:
                    pool.wait_ge(s["of_v"], i1)
                    clip(scal[:, 31, 1:2], scal[:, 31, 0:1], scal[:, 31, 2:3]).then_inc(s["oss_g"], 1)
                if L == YO:
                    pool.wait_ge(s["yo2_a"], i1)
                    clip(scal[:, 32, 1:2], scal[:, 32, 0:1], scal[:, 32, 2:3]).then_inc(s["co_g"], 1)
                if L == GATE:
                    pool.wait_ge(s["w2_a"], i1)
                    pool.wait_ge(s["wx_v"], i1)
                    mobius(sc(21), scal[:, 33, 0:1], scal[:, 33, 1:2], scal[:, 33, 2:3],
                           scal[:, 34, 0:1], scal[:, 34, 1:2], s["tm_g"], s["tm_a"], 2 * i + 1)\
                        .then_inc(s["mob_g"], 1)
                if L == X1:
                    pool.wait_ge(s["bn_v"], i1)
                    log_a(scal[:, 35, 0:1], scal[:, 35, 1:2], 1)
                    g.tensor_copy(sc(16), sc(3)).then_inc(s["th_g"], 1)
                if L == LOG_FIX + 1:
                    pool.wait_ge(s["th3_g"], i1)
                    log_b(scal[:, 35, 0:1], scal[:, 35, 1:2], scal[:, 36, 0:1], scal[:, 36, 1:2], 1)\
                        .then_inc(s["ln_g"], 1)
                if L == T2_TURN:
                    pool.wait_ge(s["t2s_a"], i1)
                    clip(scal[:, 37, 1:2], scal[:, 37, 0:1], scal[:, 37, 2:3]).then_inc(s["c2_g"], 1)
                if L == Y1B + 1:
                    pool.wait_ge(s["y1s_a"], 2 * i + 2)
                    link(g.tensor_tensor(scal[:, 38, 0:1], scal[:, 38, 0:1], scal[:, 38, 3:4], ALU.add))
                    clip(scal[:, 38, 1:2], scal[:, 38, 0:1], scal[:, 38, 2:3]).then_inc(s["c3_g"], 1)
                if L == Y2:
                    pool.wait_ge(s["y2s_a"], i1)
                    clip(scal[:, 39, 1:2], scal[:, 39, 0:1], scal[:, 39, 2:3]).then_inc(s["c4_g"], 1)
                if L == GATE2:
                    pool.wait_ge(s["w22_a"], i1)
                    pool.wait_ge(s["w2x_v"], i1)
                    mobius(sc(21), scal[:, 33, 3:4], scal[:, 33, 4:5], sc(1),
                           scal[:, 34, 2:3], scal[:, 34, 3:4], s["tm_g"], s["tm_a"], 2 * i + 2)\
                        .then_inc(s["mob2_g"], 1)

            def slot(n, t):
                parts(n, t, lambda i, l: None, post)
                if t == TOK - 1:
                    restart()

            walk(pool, slot)

        @block.scalar
        def _(act):
            a = nc.scalar
            for n, bvec in enumerate((b_q, b_k, b_v)):
                act.dma_start(bqkv[:, n * D:(n + 1) * D], rows_of(bvec).broadcast_to([P, D])).then_inc(s["b_in"], 16)
            for c in range(DC):
                act.dma_start(wada_sb[:, c, :], w_ada[c * P:(c + 1) * P, :]).then_inc(s["cond_in"], 16)
            for c in range(DC):
                act.dma_start(condT[:, c, :], cond[:, c * P:(c + 1) * P].rearrange("b p -> p b"),
                              allow_slow_non_contiguous=True).then_inc(s["cond_in"], 16)
            act.dma_start(bada_row[:], rows_of(b_ada)).then_inc(s["cond_in"], 16)
            for dst, bvec, n in ((bo, b_o, D), (bf1, b_f1, FF), (bf2, b_f2, D)):
                act.dma_start(dst[:], rows_of(bvec).broadcast_to([P, n])).then_inc(s["b_in"], 16)
            for j in range(QUAD):
                act.dma_start(bh[32 * j:32 * j + 32, :], rows_of(b_h[64 * j:64 * j + 64]).broadcast_to([32, 64]))\
                    .then_inc(s["b_in"], 16)
            act.wait_ge(s["gmem"], 3)
            hv = cond.rearrange("b (j c p) -> j c p b", c=2, p=32)
            for j in range(QUAD):
                for c in range(2):
                    act.dma_start(hist[32 * j:32 * j + 32, c, ROWS * TOK:ROWS * TOK + B], hv[j, c],
                                  allow_slow_non_contiguous=True).then_inc(s["h0_in"], 16)
            act.wait_ge(s["st_v"], 2)
            a.activation(scal[:, 6, :], scal[:, 5, :], ACT.Tanh).then_inc(s["st_a"], 1)

            with act.Fori(0, TILES // 2) as m:
                for e in range(2):
                    n1 = 2 * m + e + 1
                    if e == 0:
                        act.wait_ge(s["st_g"], 2)
                        act.wait_ge(s["t1_pe"], 2 * m)
                    a.activation(t1[:, e, :], x_all[:, bass.ds(2 * m + e, 1), :].rearrange("p a d -> p (a d)"), ACT.Identity,
                                 bias=beta_all[:, bass.ds(2 * m + e, 1)],
                                 scale=alpha_all[:, bass.ds(2 * m + e, 1)]).then_inc(s["xn_a"], 1)
                for e in range(2):
                    n1 = 2 * m + e + 1
                    act.wait_ge(s["t1_v"], n1)
                    if e == 0:
                        act.wait_ge(s["y_v"], 2 * m)
                    a.activation(junk_p[:, e * D:(e + 1) * D], t1[:, e, :], ACT.Square,
                                 accum_out=ss1[:, e:e + 1]).then_inc(s["ss_a"], 1)
                    act.wait_ge(s["t1_pe"], n1)
                    a.activation(t1T[:, e, :, :], bank[0][:, e * D:(e + 1) * D].rearrange("p (c t) -> p c t", c=DC),
                                 ACT.Copy).then_inc(s["t1T_a"], 1)
                    act.wait_ge(s["y_v"], n1)
                    a.activation(ysq[:], y[:], ACT.Square).then_inc(s["sq_a"], 1)
                    act.wait_ge(s["f_v"], n1)
                    if e == 0:
                        act.wait_ge(s["kst_pe"], 4 * m)
                    else:
                        act.wait_ge(s["kst_pe"], 4 * m + 2)
                    k_h = kf[:].rearrange("p (h o d) -> p h o d", h=H, o=1)
                    a.activation(stackb[:, :, 0:3, :], k_h.broadcast_to([P, H, 3, HD]), ACT.Copy).then_inc(s["k1_a"], 1)
                    act.wait_ge(s["r1_v"], n1)
                    r_h = resid[:].rearrange("p (h o d) -> p h o d", h=H, o=1)
                    a.activation(stackb[:, :, 3:5, :], r_h.broadcast_to([P, H, 2, HD]), ACT.Copy).then_inc(s["k2_a"], 1)
                    act.wait_ge(s["kst_pe"], 4 * m + 2 * e + 1)
                    a.activation(kT[:, 0:8, :, bass.ds((2 * m + e) * TOK, TOK)],
                                 bank[3][:].bitcast(BF16)[0:96, :].rearrange("p (h b t) -> p h b t", h=8, b=B),
                                 ACT.Copy).then_inc(s["kev_a"], 1)

            def att(i, l):
                i1 = i + 1
                if l == Q1:
                    q_h = qf[:, bass.ds(i, 1), :].rearrange("p a (h o d) -> p (a h) o d", h=H, o=1)
                    wait(act, s["qst_pe"], 2 * i)
                    a.activation(stackb[:, :, 0:4:3, :], q_h.broadcast_to([P, H, 2, HD]), ACT.Copy)
                    a.activation(stackb[:, :, 5:6, :], q_h, ACT.Copy).then_inc(s["q1_a"], 1)
                if l == Q2:
                    act.wait_ge(s["qr_v"], i1)
                    r_h = resid[:].rearrange("p (h o d) -> p h o d", h=H, o=1)
                    a.activation(stackb[:, :, 1:5:3, :], r_h.broadcast_to([P, H, 2, HD]), ACT.Copy)\
                        .then_inc(s["q2_a"], 1)
                if l in (QE, QE + 1):
                    r = 4 * (l - QE)
                    if l == QE:
                        act.wait_ge(s["qst_pe"], 2 * i + 1)
                    a.activation(qT[:, r:r + 4, :],
                                 s_bank[0][:].bitcast(BF16)[0:96, r * P:(r + 4) * P].rearrange("p (h t) -> p h t", h=4),
                                 ACT.Copy).then_inc(s["qev_a"], 1)
                for u in SCORE_UNITS.get(l - EXP_LAG, ()):
                    gb, j = u // 4, u % 4
                    act.wait_ge(s["s_pe"], 32 * i + u + 1)
                    if j == 0:
                        wait(act, s["pv_pe"], 8 * i + gb - 1)
                    a.activation(probs[:, gb % 2, j, :], s_bank[u % 2][:, :], ACT.Exp).then_inc(s["p_a"], 1)

            def post(i, L):
                i1 = i + 1
                if L == O_COPY:
                    act.wait_ge(s["pv_pe"], 8 * i + 8)
                    a.activation(oT[:], o_bank[:, :], ACT.Copy).then_inc(s["o_ev"], 1)
                if L == O_SQUARE:
                    act.wait_ge(s["to_pe"], i1)
                    to = a_bank[:].rearrange("p (h r) -> p h r", h=H)
                    a.activation(junk_a[:, 0:D].rearrange("p (h d) -> p h d", h=H), to[:, :, 0:HD], ACT.Square)\
                        .then_inc(s["osq_a"], 1)
                if L == Z_COPY:
                    act.wait_ge(s["z_pe"], i1)
                    a.activation(aT[:], a_bank[:, 0:D].rearrange("p (c t) -> p c t", c=DC), ACT.Copy)\
                        .then_inc(s["zc_a"], 1)
                if L == WO:
                    act.wait_ge(s["xin_in"], 32 * i + 32)
                    a.activation(junk_a[:, 256:512], xin[:], ACT.Square, accum_out=scal[:, 33, 2:3])
                if L == YO:
                    act.wait_ge(s["yo_v"], i1)
                    a.activation(junk_a[:, 512:768], wa[:], ACT.Square, accum_out=scal[:, 32, 0:1])\
                        .then_inc(s["yo2_a"], 1)
                if L == GATE:
                    act.wait_ge(s["w_v"], i1)
                    a.activation(junk_a[:, 768:1024], wb[:], ACT.Square, accum_out=scal[:, 33, 0:1])\
                        .then_inc(s["w2_a"], 1)
                if L == MOB_TANH:
                    act.wait_ge(s["tm_g"], 2 * i + 1)
                    a.activation(scal[:, 21, 0:1], scal[:, 20, 0:1], ACT.Tanh).then_inc(s["tm_a"], 1)
                if L == LOG_TANH:
                    act.wait_ge(s["th_a"], i1)
                    a.activation(scal[:, 6, 0:1], scal[:, 5, 0:1], ACT.Tanh).then_inc(s["th2_a"], 1)
                if L == NORM:
                    act.wait_ge(s["ln_g"], i1)
                    a.activation(wa[:], x1[:], ACT.Identity, bias=scal[:, 36, 1:2], scale=scal[:, 36, 0:1])\
                        .then_inc(s["xn2_a"], 1)
                if L == T2_TURN:
                    act.wait_ge(s["t2_v"], i1)
                    a.activation(junk_a[:, 0:256], wb[:], ACT.Square, accum_out=scal[:, 37, 0:1])\
                        .then_inc(s["t2s_a"], 1)
                if L == T2_TURN + 1:
                    act.wait_ge(s["t2_pe"], i1)
                    a.activation(aT[:], a_bank[:, 0:D].rearrange("p (c t) -> p c t", c=DC), ACT.Copy)\
                        .then_inc(s["t2T_a"], 1)
                if L == Y1A + 1:
                    act.wait_ge(s["y1_v"], 2 * i + 1)
                    a.activation(junk_a[:, 0:512], y1[:, 0:512], ACT.Square, accum_out=scal[:, 38, 0:1])\
                        .then_inc(s["y1s_a"], 1)
                if L == Y1B + 1:
                    act.wait_ge(s["y1_v"], 2 * i + 2)
                    a.activation(junk_a[:, 512:1024], y1[:, 512:1024], ACT.Square, accum_out=scal[:, 38, 3:4])\
                        .then_inc(s["y1s_a"], 1)
                for half, at, bk in ((0, Y1_COPY[0], a_bank), (1, Y1_COPY[1], b_bank)):
                    if L == at:
                        act.wait_ge(s["y1_pe"], 2 * i + half + 1)
                        a.activation(y1T[:, 4 * half:4 * half + 4, :], bk[:].rearrange("p (c t) -> p c t", c=4),
                                     ACT.Copy).then_inc(s["y1T_a"], 1)
                if L == Y2:
                    act.wait_ge(s["y2_v"], i1)
                    a.activation(junk_a[:, 256:512], wa[:], ACT.Square, accum_out=scal[:, 39, 0:1])\
                        .then_inc(s["y2s_a"], 1)
                if L == GATE2:
                    act.wait_ge(s["w2_v"], i1)
                    a.activation(junk_a[:, 512:768], wb[:], ACT.Square, accum_out=scal[:, 33, 3:4])\
                        .then_inc(s["w22_a"], 1)
                if L == MOB2_TANH:
                    act.wait_ge(s["tm_g"], 2 * i + 2)
                    a.activation(scal[:, 21, 0:1], scal[:, 20, 0:1], ACT.Tanh).then_inc(s["tm_a"], 1)
                if L == XO_TURN + 1:
                    act.wait_ge(s["xo_pe"], i1)
                    a.activation(xT[:].rearrange("p c (t b) -> p c b t", b=B),
                                 m_bank[:, 0:D].rearrange("p (c b t) -> p c b t", c=DC, b=B), ACT.Copy)\
                        .then_inc(s["xT_a"], 1)

            def rnn_step(n, t):
                m = t % BLK
                z = z_bank[(t // BLK) % 2]
                act.wait_ge(s["tr_v"], n * TOK + t + 1)
                a.activation(hist[:, :, ROWS * (t + 1):ROWS * (t + 1) + B],
                             z[:, 64:128].rearrange("p (c r) -> p c r", c=2)[:, :, B * m:B * m + B],
                             ACT.Tanh).then_inc(s["h_a"], 1)

            def slot(n, t):
                if live(n):
                    rnn_step(n, t)
                parts(n, t, att, post)

            act.wait_ge(s["h0_in"], 16 * 2 * QUAD)
            act.nop().then_inc(s["h_a"], 1)
            act.wait_ge(s["kst_pe"], 2 * TILES)
            walk(act, slot)

        @block.vector
        def _(dve):
            v = nc.vector
            link, then, last, restart = chain(dve, dve_link)
            restart()
            dve.wait_ge(s["gmem"], 3)
            dve.wait_ge(s["gconst"], 5)
            v.tensor_copy(ident_bf[:], ident[:]).then_inc(s["cond_spread"], 1)
            for j in range(QUAD):
                for c in range(2):
                    o = 64 * j + 32 * c
                    v.tensor_copy(perm[32 * j:32 * j + 32, c, o:o + 32],
                                  ident[32 * j:32 * j + 32, 32 * j:32 * j + 32]).then_inc(s["cond_spread"], 1)
            dve.wait_ge(s["cond_in"], 80)
            for c in range(DC):
                for b in range(B):
                    v.tensor_scalar(cond_rows[:, c, b * TOK:(b + 1) * TOK], ident[:, 0:TOK], 0.0, condT[:, c, b:b + 1],
                                    ALU.mult, ALU.add).then_inc(s["cond_spread"], 1)
            dve.wait_ge(s["x_in"], 64)
            link(v.memset(o_bank[:, :], 0.0))
            for i in range(TILES):
                link(v.bn_stats(bns[:], x_all[:, i, :]))
                link(v.bn_aggr(bna[:, i, :], bns[:]))
            v.engine_nop().then_inc(s["st_v"], 1)

            dve.wait_ge(s["ada_done"], 1)
            for n in range(3):
                v.tensor_copy(mod[:, n * 512:(n + 1) * 512], bank[n][:, :]).then_inc(s["mod_done"], 1)
            dve.wait_ge(s["mod_done"], 3)
            for n in (1, 4):
                v.tensor_scalar(mod[:, n * D:(n + 1) * D], mod[:, n * D:(n + 1) * D], 1.0, None, ALU.add)\
                    .then_inc(s["mod_done"], 1)
            dve.wait_ge(s["mod_done"], 5)

            def sc(k, n=1):
                return scal[:, k, 0:n]

            def guess(n):
                link(v.tensor_scalar(sc(4, n), sc(16, n), -1.0, 1.0, ALU.mult, ALU.add))
                link(v.reciprocal(sc(4, n), sc(4, n)))
                link(v.scalar_tensor_tensor(sc(4, n), sc(16, n), 1.0, sc(4, n), ALU.add, ALU.mult))
                return v.tensor_scalar(sc(5, n), sc(4, n).bitcast(I32), ONE_BITS, LOG_STEP, ALU.subtract, ALU.mult)

            def correct(n, part):
                if part == 0:
                    link(v.tensor_tensor(sc(7, n), sc(16, n), sc(6, n), ALU.mult))
                    link(v.tensor_scalar(sc(7, n), sc(7, n), -1.0, 1.0, ALU.mult, ALU.add))
                    link(v.reciprocal(sc(7, n), sc(7, n)))
                    return None
                link(v.tensor_tensor(sc(8, n), sc(16, n), sc(6, n), ALU.subtract))
                link(v.tensor_tensor(sc(8, n), sc(8, n), sc(7, n), ALU.mult))
                return v.reciprocal(sc(13, n), sc(2, n))

            dve.wait_ge(s["st_g"], 1)
            guess(TILES).then_inc(s["st_v"], 1)
            dve.wait_ge(s["st_a"], 1)
            correct(TILES, 0)
            correct(TILES, 1).then_inc(s["st_n"], 2)

            def rsqrt(y_, x_, t_, bits):
                link(v.tensor_scalar(bits, x_.bitcast(I32), 1, None, ALU.logical_shift_right))
                link(v.tensor_scalar(y_.bitcast(I32), bits, -1.0, MAGIC, ALU.mult, ALU.add))
                for _ in range(3):
                    link(v.scalar_tensor_tensor(t_, y_, -0.5, y_, ALU.mult, ALU.mult))
                    link(v.tensor_tensor(t_, t_, x_, ALU.mult))
                    link(v.scalar_tensor_tensor(y_, t_, 1.5, y_, ALU.add, ALU.mult))

            N = 3 * H
            restart()
            with dve.Fori(0, TILES // 2) as m:
                for e in range(2):
                    n1 = 2 * m + e + 1
                    dve.wait_ge(s["xn_a"], n1)
                    link(v.tensor_tensor(t1[:, e, :], t1[:, e, :], mod[:, D:2 * D], ALU.mult))
                    v.tensor_tensor(t1[:, e, :], t1[:, e, :], mod[:, 0:D], ALU.add).then_inc(s["t1_v"], 1)
                for e in range(2):
                    n1 = 2 * m + e + 1
                    dve.wait_ge(s["c1_g"], n1)
                    dve.wait_ge(s["qkv_pe"], n1)
                    dve.wait_ge(s["b_in"], 16 * 10)
                    v.scalar_tensor_tensor(y[:, 0:512], bank[1][:, :], c1[:, e:e + 1], bqkv[:, 0:512],
                                           ALU.mult, ALU.add)
                    v.scalar_tensor_tensor(y[:, 512:768], bank[2][:, 0:D], c1[:, e:e + 1], bqkv[:, 512:768],
                                           ALU.mult, ALU.add).then_inc(s["y_v"], 1)
                    dve.wait_ge(s["sq_a"], n1)
                    link(v.tensor_reduce(nw[:, 0, 0:N], ysq[:].rearrange("p (h d) -> p h d", d=HD), AX_X, ALU.add))
                    link(v.tensor_reduce(nw[:, 0, N:N + 3], nw[:, 0, 0:N].rearrange("p (n h) -> p n h", n=3), AX_X, ALU.add))
                    link(v.tensor_scalar(nw[:, 0, :], nw[:, 0, :], TINY, None, ALU.max))
                    rsqrt(nw[:, 1, :], nw[:, 0, :], nw[:, 2, :], nw[:, 3, :].bitcast(I32))
                    link(v.tensor_scalar(fac3[:], nw[:, 1, N:N + 3], RHO * RADIUS, RHO, ALU.mult, ALU.min))
                    link(v.scalar_tensor_tensor(fac[:], nw[:, 1, 0:N].rearrange("p (n h) -> p n h", n=3), RADIUS,
                                                fac3[:].rearrange("p (n o) -> p n o", o=1).broadcast_to([P, 3, H]),
                                                ALU.mult, ALU.min))
                    link(v.tensor_scalar(fac[:, 0, :], fac[:, 0, :], 1.0 / math.sqrt(HD), None, ALU.mult))

                    def head(ap, n, r0=0, r1=P):
                        return (ap[r0:r1, n * D:(n + 1) * D].rearrange("p (h d) -> p h d", h=H),
                                fac[r0:r1, n, :].rearrange("p (h o) -> p h o", o=1).broadcast_to([r1 - r0, H, HD]))
                    yk, fk = head(y, 1)
                    dve.wait_ge(s["k1_a"], 2 * m + e)
                    v.tensor_tensor(kf[:].rearrange("p (h d) -> p h d", h=H), yk, fk, ALU.mult).then_inc(s["f_v"], 1)
                    yq, fq = head(y, 0)
                    v.tensor_tensor(qf[:, bass.ds(2 * m + e, 1), :].rearrange("p a (h d) -> p (a h) d", h=H), yq, fq, ALU.mult)
                    for b in range(B):
                        yv, fv = head(y, 2, b * TOK, (b + 1) * TOK)
                        v.tensor_tensor(vals[e * TOK:(e + 1) * TOK, bass.ds(m, 1), b, :, 0:HD]
                                        .rearrange("p a h d -> p (a h) d"),
                                        yv, fv, ALU.mult).then_inc(s["v_v"], 1)
                    dve.wait_ge(s["k1_a"], n1)
                    v.tensor_tensor(resid[:].rearrange("p (h d) -> p h d", h=H), kf[:].rearrange("p (h d) -> p h d", h=H),
                                    stackb[:, :, 0, :], ALU.subtract).then_inc(s["r1_v"], 1)
                    dve.wait_ge(s["k2_a"], n1)
                    v.tensor_tensor(stackb[:, :, 5, :], resid[:].rearrange("p (h d) -> p h d", h=H),
                                    stackb[:, :, 3, :], ALU.subtract).then_inc(s["k3_v"], 1)
                    dve.wait_ge(s["kst_pe"], 4 * m + 2 * e + 2)
                    v.tensor_copy(kT[:, 8:16, :, bass.ds((2 * m + e) * TOK, TOK)],
                                  bank[4][:].bitcast(BF16)[0:96, :].rearrange("p (h b t) -> p h b t", h=8, b=B))\
                        .then_inc(s["kev_v"], 1)
                restart()

            def att(i, l):
                i1 = i + 1
                r = resid[:].rearrange("p (h d) -> p h d", h=H)
                if l == Q1 + 1:
                    dve.wait_ge(s["q1_a"], i1)
                    v.tensor_tensor(r, qf[:, bass.ds(i, 1), :].rearrange("p a (h d) -> p (a h) d", h=H),
                                    stackb[:, :, 0, :], ALU.subtract).then_inc(s["qr_v"], 1)
                if l == Q3:
                    dve.wait_ge(s["q2_a"], i1)
                    v.tensor_tensor(stackb[:, :, 2, :], r, stackb[:, :, 1, :], ALU.subtract).then_inc(s["q3_v"], 1)
                if l in (QE, QE + 1):
                    o = 4 * (l - QE)
                    if l == QE:
                        dve.wait_ge(s["qst_pe"], 2 * i + 2)
                    v.tensor_copy(qT[:, 8 + o:12 + o, :], s_bank[1][:].bitcast(BF16)[0:96, o * P:(o + 4) * P]
                                  .rearrange("p (h t) -> p h t", h=4)).then_inc(s["qev_v"], 1)

            def heads(i, part):
                to = a_bank[:].rearrange("p (h r) -> p h r", h=H)
                rec, ssq = fac[:, 0, :], fac[:, 1, :]
                n2, r_, t_, bits = nw[:, 0, 0:H], nw[:, 1, 0:H], nw[:, 2, 0:H], nw[:, 3, 0:H].bitcast(I32)
                if part == 0:
                    dve.wait_ge(s["osq_a"], i + 1)
                    then(v.reciprocal(rec, to[:, :, HD]))
                    then(v.tensor_reduce(ssq, junk_a[:, 0:D].rearrange("p (h d) -> p h d", h=H), AX_X, ALU.add))
                    last()
                    then(v.scalar_tensor_tensor(n2, ssq, TINY, rec, ALU.add, ALU.mult))
                    last()
                    then(v.scalar_tensor_tensor(n2, n2, TINY, rec, ALU.add, ALU.mult))
                if part == 1:
                    last()
                    then(v.tensor_scalar(bits, n2.bitcast(I32), 1, None, ALU.logical_shift_right))
                    last()
                    then(v.tensor_scalar(r_.bitcast(I32), bits, -1.0, MAGIC, ALU.mult, ALU.add))
                if part in (2, 3, 4):
                    last()
                    then(v.scalar_tensor_tensor(t_, r_, -0.5, r_, ALU.mult, ALU.mult))
                    last()
                    then(v.tensor_tensor(t_, t_, n2, ALU.mult))
                    last()
                    then(v.scalar_tensor_tensor(r_, t_, 1.5, r_, ALU.add, ALU.mult))
                if part == 5:
                    last()
                    then(v.tensor_scalar(r_, r_, RADIUS / RHO, 1.0 / RHO, ALU.mult, ALU.min))
                    last()
                    then(v.tensor_tensor(t_, r_, r_, ALU.mult))
                    then(v.tensor_tensor(ssq, r_, rec, ALU.mult))
                    last()
                    then(v.tensor_tensor(t_, t_, n2, ALU.mult))
                    last()
                    v.tensor_reduce(scal[:, 31, 0:1], t_, AX_X, ALU.add).then_inc(s["of_v"], 1)
                if part == 6:
                    v.tensor_tensor(wc[:].rearrange("p (h d) -> p h d", h=H), to[:, :, 0:HD],
                                    ssq.rearrange("p (h o) -> p h o", o=1).broadcast_to([P, H, HD]),
                                    ALU.mult).then_inc(s["zt_v"], 1)

            def post(i, L):
                i1 = i + 1
                if HEADS <= L < HEADS + 7:
                    heads(i, L - HEADS)
                if L == YO:
                    dve.wait_ge(s["wo_pe"], i1)
                    dve.wait_ge(s["oss_g"], i1)
                    v.scalar_tensor_tensor(wa[:], b_bank[:, 0:D], scal[:, 31, 1:2], bo[:], ALU.mult, ALU.add)\
                        .then_inc(s["yo_v"], 1)
                if L == GATE:
                    dve.wait_ge(s["co_g"], i1)
                    v.scalar_tensor_tensor(wb[:], wa[:], scal[:, 32, 1:2], mod[:, 2 * D:3 * D], ALU.mult, ALU.mult)\
                        .then_inc(s["w_v"], 1)
                    dve.wait_ge(s["w_v"], i1)
                    dve.wait_ge(s["xin_in"], 32 * i + 32)
                    v.tensor_tensor_reduce(junk_v[:], wb[:], xin[:], 1.0, 0.0, ALU.mult, ALU.add, scal[:, 33, 1:2])\
                        .then_inc(s["wx_v"], 1)
                if L == X1:
                    dve.wait_ge(s["mob_g"], i1)
                    then(v.tensor_scalar(wb[:], wb[:], scal[:, 34, 1:2], None, ALU.mult))
                    last()
                    then(v.scalar_tensor_tensor(x1[:], xin[:], scal[:, 34, 0:1], wb[:], ALU.mult, ALU.add))
                if L == X1 + 1:
                    last()
                    then(v.bn_stats(bns[:], x1[:]))
                    last()
                    v.bn_aggr(scal[:, 35, 0:2], bns[:]).then_inc(s["bn_v"], 1)
                if L == LOG_GUESS:
                    dve.wait_ge(s["th_g"], i1)
                    guess(1).then_inc(s["th_a"], 1)
                if L == LOG_FIX:
                    dve.wait_ge(s["th2_a"], i1)
                    correct(1, 0)
                if L == LOG_FIX + 1:
                    correct(1, 1).then_inc(s["th3_g"], 1)
                if L == T2:
                    dve.wait_ge(s["xn2_a"], i1)
                    then(v.tensor_tensor(wb[:], wa[:], mod[:, 4 * D:5 * D], ALU.mult))
                    last()
                    v.tensor_tensor(wb[:], wb[:], mod[:, 3 * D:4 * D], ALU.add).then_inc(s["t2_v"], 1)
                for half, at, bk in ((0, Y1A, a_bank), (1, Y1B, b_bank)):
                    if L == at:
                        dve.wait_ge(s["c2_g"], i1)
                        dve.wait_ge(s["f1_pe"], 2 * i + half + 1)
                        o = 512 * half
                        v.scalar_tensor_tensor(y1[:, o:o + 512], bk[:, :], scal[:, 37, 1:2], bf1[:, o:o + 512],
                                               ALU.mult, ALU.add).then_inc(s["y1_v"], 1)
                if L == Y2:
                    dve.wait_ge(s["c3_g"], i1)
                    dve.wait_ge(s["f2_pe"], i1)
                    v.scalar_tensor_tensor(wa[:], m_bank[:, 256:512], scal[:, 38, 1:2], bf2[:], ALU.mult, ALU.add)\
                        .then_inc(s["y2_v"], 1)
                if L == GATE2:
                    dve.wait_ge(s["c4_g"], i1)
                    v.scalar_tensor_tensor(wb[:], wa[:], scal[:, 39, 1:2], mod[:, 5 * D:6 * D], ALU.mult, ALU.mult)\
                        .then_inc(s["w2_v"], 1)
                    dve.wait_ge(s["w2_v"], i1)
                    v.tensor_tensor_reduce(junk_v[:], wb[:], x1[:], 1.0, 0.0, ALU.mult, ALU.add, scal[:, 33, 4:5])\
                        .then_inc(s["w2x_v"], 1)
                if L == XO:
                    dve.wait_ge(s["mob2_g"], i1)
                    wait(dve, s["x_held"], 16 * i)
                    then(v.tensor_scalar(wb[:], wb[:], scal[:, 34, 3:4], None, ALU.mult))
                if L == XO + 1:
                    last()
                    then(v.scalar_tensor_tensor(wb[:], x1[:], scal[:, 34, 2:3], wb[:], ALU.mult, ALU.add))
                if L == XO + 2:
                    last()
                    v.tensor_tensor(xo[:], wb[:], xin[:], ALU.add).then_inc(s["xo_v"], 1)

            def rnn_step(n, t):
                z = z_bank[(t // BLK) % 2]
                dve.wait_ge(s["z_pe_step"], n * TOK + t + 1)
                v.transpose(z[:, 64:128], z[:, 0:64]).then_inc(s["tr_v"], 1)

            def store(n, hh):
                dve.wait_ge(s["flush_pe"], 2 * n + hh + 1)
                wait(dve, s["out_dma"], 32 * (2 * n + hh - 1))
                dve.wait_ge(s["x_held"], 16 * (n + 1))
                for b in range(B):
                    q = b * TOK + HALF * hh
                    ins = v.tensor_tensor(oat[q:q + HALF, :], m_bank[q:q + HALF, 0:D], xhold[q:q + HALF, :], ALU.add)
                ins.then_inc(s["out_v"], 1)

            def bias(n, k):
                if isinstance(n, int) and n == 0 and k < 2:
                    dve.wait_ge(s["bits_pe"], 2)
                else:
                    dve.wait_ge(s["h_a"], n * TOK + (k - 1) * BLK + 1)
                v.tensor_copy(z_bank[k % 2][:, 0:64], bh[:]).then_inc(s["bias_v"], 1)

            def slot(n, t):
                if live(n):
                    rnn_step(n, t)
                if live(n) and t % BLK == BIAS and t // BLK + 1 < TOK // BLK:
                    bias(n, t // BLK + 1)
                if live(n + 1) and t == FIRST_INPUTS - 1:
                    bias(n + 1, 0)
                if live(n):
                    if t == FLUSH[0] + 3:
                        store(n, 0)
                if t == FLUSH[1] + 3 and (not isinstance(n, int) or 1 <= n <= TILES):
                    store(n - 1, 1)
                parts(n, t, att, post)
                if t == TOK - 1:
                    restart()

            walk(dve, slot)

        @block.tensor
        def _(pe):
            t_ = nc.tensor
            pe.wait_ge(s["cond_spread"], 13)
            pe.wait_ge(s["cond_in"], 80)
            pe.wait_ge(s["gconst"], 5)
            for n in range(3):
                for c in range(DC):
                    t_.matmul(bank[n][:, :], cond_rows[:, c, :], wada_sb[:, c, n * 512:(n + 1) * 512],
                              start=(c == 0), stop=False)
                mm = t_.matmul(bank[n][:, :], ones_row[:], bada_row[:, n * 512:(n + 1) * 512], start=False, stop=True)
            mm.then_inc(s["ada_done"], 1)
            pe.wait_ge(s["mod_done"], 5)
            pe.wait_ge(s["w_in"], 16 * 11)

            def turn(dst, src, chunks):
                for c in chunks:
                    mm = t_.transpose(dst[:, c * P:(c + 1) * P], src[:, c * P:(c + 1) * P], ident[:])
                return mm

            def stack_turn(half, bk):
                dst = bk[:].bitcast(BF16)
                for h in range(8):
                    mm = t_.transpose(dst[0:96, h * P:(h + 1) * P],
                                      stackb[:, 8 * half + h, :, :].rearrange("p a d -> p (a d)"), ident_bf[:])
                return mm

            with pe.Fori(0, TILES // 2) as m:
                for e in range(2):
                    n1 = 2 * m + e + 1
                    pe.wait_ge(s["t1_v"], n1)
                    if e == 0:
                        pe.wait_ge(s["t1T_a"], 2 * m)
                    else:
                        pe.wait_ge(s["t1T_a"], 2 * m + 1)
                    turn(bank[0][:, e * D:(e + 1) * D], t1[:, e, :], range(DC)).then_inc(s["t1_pe"], 1)
                    pe.wait_ge(s["t1T_a"], n1)
                    pe.wait_ge(s["y_v"], 2 * m + e)
                    for c in range(DC):
                        t_.matmul(bank[1][:, :], t1T[:, e, c, :], wqkv[:, c, 0:512], start=(c == 0), stop=(c == DC - 1))
                    for c in range(DC):
                        mm = t_.matmul(bank[2][:, 0:D], t1T[:, e, c, :], wqkv[:, c, 512:768],
                                       start=(c == 0), stop=(c == DC - 1))
                    mm.then_inc(s["qkv_pe"], 1)
                    pe.wait_ge(s["k3_v"], n1)
                    pe.wait_ge(s["kev_a"], 2 * m + e)
                    stack_turn(0, bank[3]).then_inc(s["kst_pe"], 1)
                    pe.wait_ge(s["kev_v"], 2 * m + e)
                    stack_turn(1, bank[4]).then_inc(s["kst_pe"], 1)

            def att(i, l):
                i1 = i + 1
                if l == QT:
                    pe.wait_ge(s["q3_v"], i1)
                    wait(pe, s["p_a"], 32 * i)
                    stack_turn(0, s_bank[0]).then_inc(s["qst_pe"], 1)
                if l == QT + 1:
                    stack_turn(1, s_bank[1]).then_inc(s["qst_pe"], 1)
                for u in SCORE_UNITS.get(l, ()):
                    g, b, j = u // 8, (u // 4) % 2, u % 4
                    h = QUAD * g + j
                    if u == 0:
                        pe.wait_ge(s["qev_a"], 2 * i1)
                        pe.wait_ge(s["qev_v"], 2 * i1)
                    if u >= 2:
                        pe.wait_ge(s["p_a"], 32 * i + u - 1)
                    for kc in range(KC):
                        mm = t_.matmul(s_bank[u % 2][:, kc * TOK:(kc + 1) * TOK], kT[:, h, b, kc * P:(kc + 1) * P],
                                       qT[:, h, b * TOK:(b + 1) * TOK], start=(kc == 0), stop=(kc == KC - 1),
                                       skip_group_check=True)
                    mm.then_inc(s["s_pe"], 1)
                for k in OUTPUT_CHUNKS.get(l, ()):
                    w, kc = k // KC, k % KC
                    g, b = w // 2, w % 2
                    if kc == 0:
                        pe.wait_ge(s["p_a"], 32 * i + 4 * w + 4)
                        if w == 0:
                            wait(pe, s["o_ev"], i)
                    for j in range(QUAD):
                        mm = t_.matmul(o_bank[32 * j:32 * j + HD + 1, w * TOK:(w + 1) * TOK],
                                       vals[:, kc, b, QUAD * g + j, :], probs[:, w % 2, j, kc * TOK:(kc + 1) * TOK],
                                       start=(kc == 0), stop=(kc == KC - 1), skip_group_check=True)
                    if kc == KC - 1:
                        mm.then_inc(s["pv_pe"], 1)

            def post(i, L):
                i1 = i + 1
                if L == O_TURN:
                    pe.wait_ge(s["o_ev"], i1)
                    wait(pe, s["y1T_a"], 2 * i)
                    turn(a_bank, oT, range(0, 2))
                if L == O_TURN + 1:
                    turn(a_bank, oT, range(2, 4)).then_inc(s["to_pe"], 1)
                if L == Z_TURN:
                    pe.wait_ge(s["zt_v"], i1)
                    turn(a_bank, wc, range(DC)).then_inc(s["z_pe"], 1)
                if WO <= L < WO + DC:
                    c = L - WO
                    if c == 0:
                        pe.wait_ge(s["zc_a"], i1)
                    mm = t_.matmul(b_bank[:, 0:D], aT[:, c, :], wo[:, c, :], start=(c == 0), stop=(c == DC - 1))
                    if c == DC - 1:
                        mm.then_inc(s["wo_pe"], 1)
                if L == T2_TURN:
                    pe.wait_ge(s["t2_v"], i1)
                    turn(a_bank, wb, range(DC)).then_inc(s["t2_pe"], 1)
                if F1 <= L < F1 + FC:
                    n = L - F1
                    if n == 0:
                        pe.wait_ge(s["t2T_a"], i1)
                    bk, o = (a_bank, b_bank)[n // 4], P * (n % 4)
                    for c in range(DC):
                        mm = t_.matmul(bk[:, o:o + P], aT[:, c, :], wf1[:, c, n * P:(n + 1) * P],
                                       start=(c == 0), stop=(c == DC - 1))
                    if n % 4 == 3:
                        mm.then_inc(s["f1_pe"], 1)
                for half, at in enumerate(Y1_TURN):
                    if at <= L < at + 2:
                        c = 2 * (L - at)
                        if c == 0:
                            pe.wait_ge(s["y1_v"], 2 * i + half + 1)
                        mm = turn((a_bank, b_bank)[half], y1[:, 512 * half:512 * half + 512], range(c, c + 2))
                        if c:
                            mm.then_inc(s["y1_pe"], 1)
                if F2 <= L < F2 + FC:
                    c = L - F2
                    if c % 4 == 0:
                        pe.wait_ge(s["y1T_a"], 2 * i + c // 4 + 1)
                    mm = t_.matmul(m_bank[:, 256:512], y1T[:, c, :], wf2[:, c, :], start=(c == 0), stop=(c == FC - 1))
                    if c == FC - 1:
                        mm.then_inc(s["f2_pe"], 1)
                if L == XO_TURN:
                    pe.wait_ge(s["xo_v"], i1)
                    turn(m_bank, xo, range(DC)).then_inc(s["xo_pe"], 1)

            def inputs(k, part):
                z = z_bank[k % 2]
                for j in range(QUAD):
                    dst, cols = z[32 * j:32 * j + ROWS, 0:64], slice(64 * j, 64 * j + 64)
                    t_.matmul(dst, xT[:, part, ROWS * k:ROWS * (k + 1)], wx[:, part, cols], start=False, stop=False,
                              skip_group_check=True)

            def rnn_step(n, t):
                m = t % BLK
                z = z_bank[(t // BLK) % 2]
                base = ROWS * (t if t else TOK) - B * m
                pe.wait_ge(s["h_a"], n * TOK + t + 1)
                for c in range(2):
                    for j in range(QUAD):
                        mm = t_.matmul(z[32 * j:32 * j + ROWS, 0:64], hist[:, c, base:base + ROWS],
                                       wh[:, c, 64 * j:64 * j + 64], start=False, stop=(c == 1 and m == BLK - 1),
                                       skip_group_check=True)
                mm.then_inc(s["z_pe_step"], 1)

            def fill(bk, first, last, start):
                n = last - first
                return t_.matmul(bk[:, P * first:P * last].rearrange("p (a n) -> p a n", a=n), ident_bf[:],
                                 ident_bf[:].rearrange("p (a n) -> p a n", a=1).broadcast_to([P, n, P]),
                                 start=start, stop=False, skip_group_check=True)

            def keep_clock(t, n):
                fill(z_bank[(t // BLK + 1) % 2], 1, 1 + n, False)

            def flush(hh, c):
                for b in range(B):
                    o = ROWS * (HALF * hh + 1)
                    hs = hist[:, c, o:o + ROWS * HALF].rearrange("p (s r) -> p s r", r=ROWS)[:, :, b]
                    q = b * TOK + HALF * hh
                    mm = t_.matmul(m_bank[q:q + HALF, 0:D], hs, perm[:, c, :], start=(c == 0), stop=(c == 1),
                                   skip_group_check=True)
                if c == 1:
                    mm.then_inc(s["flush_pe"], 1)

            def slot(n, t):
                if live(n):
                    rnn_step(n, t)
                    part = t % BLK - INPUTS
                    if 0 <= part < DC and t // BLK + 1 < TOK // BLK:
                        if part == 0:
                            pe.wait_ge(s["bias_v"], TOK // BLK * n + t // BLK + 2)
                        inputs(t // BLK + 1, part)
                    if t in (FLUSH[0], FLUSH[0] + 1):
                        if t == FLUSH[0]:
                            pe.wait_ge(s["xT_a"], n + 1)
                        flush(0, t - FLUSH[0])
                if t in (FLUSH[1], FLUSH[1] + 1) and (not isinstance(n, int) or 1 <= n <= TILES):
                    if t == FLUSH[1]:
                        if not live(n):
                            pe.wait_ge(s["h_a"], TILES * TOK + 1)
                            pe.wait_ge(s["xT_a"], TILES)
                        else:
                            pe.wait_ge(s["xT_a"], n + 1)
                        pe.wait_ge(s["out_v"], 2 * n - 1)
                    flush(1, t - FLUSH[1])
                if live(n) and t % BLK != BIAS and t not in (FIRST_INPUTS - 1, FIRST_INPUTS):
                    if isinstance(n, int) and n >= TILES - 2:
                        keep_clock(t, 3)
                        keep_clock(t, 3)
                    elif LOAD[(t + LEAD) % TOK] < CLOCK_LOAD:
                        keep_clock(t, FILL)
                parts(n, t, att, post)
                if live(n + 1) and FIRST_INPUTS <= t < FIRST_INPUTS + DC:
                    if t == FIRST_INPUTS:
                        pe.wait_ge(s["xT_a"], n + 2)
                        pe.wait_ge(s["bias_v"], TOK // BLK * (n + 1) + 1)
                    inputs(0, t - FIRST_INPUTS)

            pe.wait_ge(s["kev_a"], TILES)
            pe.wait_ge(s["kev_v"], TILES)
            pe.wait_ge(s["v_v"], 2 * TILES)
            for z in z_bank:
                fill(z, 0, 4, True).then_inc(s["bits_pe"], 1)
            walk(pe, slot)


_INS = ['x', 'cond_1024', 'L0_cond_w_q', 'L0_cond_b_q', 'L0_cond_w_k', 'L0_cond_b_k', 'L0_cond_w_v', 'L0_cond_b_v',
        'L0_cond_w_o', 'L0_cond_b_o', 'L0_cond_w_f1', 'L0_cond_b_f1', 'L0_cond_w_f2', 'L0_cond_b_f2',
        'L0_cond_w_ada', 'L0_cond_b_ada', 'L1_cond_Wx', 'L1_cond_Wh', 'L1_cond_b']


def kernel(**inputs):
    import numpy as _np
    import concourse.bacc as _bacc
    from concourse import mybir as _mybir
    from concourse.bass_utils import run_bass_kernel_spmd as _run

    nc = _bacc.Bacc("TRN2", target_bir_lowering=False, num_devices=1)
    arrays, args = {}, []
    for name in _INS:
        a = _np.ascontiguousarray(inputs[name])
        arrays[f"in_{name}_dram"] = a
        args.append(nc.dram_tensor(f"in_{name}_dram", a.shape, _mybir.dt.from_np(a.dtype), kind="ExternalInput").ap())
    args.append(nc.dram_tensor("out_0_dram", (2, 1024, 256), _mybir.dt.float32, kind="ExternalOutput").ap())
    build(nc, *args)
    r = _run(nc, [arrays], core_ids=[0])
    return r.results[0]["out_0_dram"]
```

```python
import math
from contextlib import ExitStack

import numpy as np

import concourse.bass as bass
from concourse import mybir

F32 = mybir.dt.float32
BF16 = mybir.dt.bfloat16
I32 = mybir.dt.int32
ALU = mybir.AluOpType
ACT = mybir.ActivationFunctionType
AX_X = mybir.AxisListType.X

P = 128
B, S, D = 2, 1024, 256
H, HD, FF = 16, 16, 1024
TOK = P // B
TILES = S // TOK
DC = D // P
FC = FF // P
KC = S // P
PARTS = 6
QUAD = 4
BLK = 8
ROWS = B * BLK
HALF = TOK // 2

LEAD = 12
LOOP = (1, TILES - 3)

PREP_FILL = 14
PAIRS = TILES // 2


def pairs(eng, step):
    step(0, 2)
    with eng.Fori(1, PAIRS - 2) as m:
        step(m, 2)
    step(PAIRS - 2, 1)
    step(PAIRS - 1, 0)


def live(tile):
    return not isinstance(tile, int) or 0 <= tile < TILES


def wait(eng, semaphore, value):
    if not isinstance(value, int) or value > 0:
        eng.wait_ge(semaphore, value)


def walk(eng, slot):
    for n in range(-3, LOOP[0]):
        for t in range(TOK):
            slot(n, t)
    with eng.Fori(*LOOP) as n:
        for t in range(TOK):
            slot(n, t)
    for n in range(LOOP[1], TILES + 1):
        for t in range(TOK):
            slot(n, t)


def parts(n, t, att, post):
    if t < TOK - LEAD and live(n + 2):
        att(n + 2, t + LEAD)
    if t >= TOK - LEAD + Q1 and live(n + 3):
        att(n + 3, t + LEAD - TOK)
    if live(n + 1):
        post(n + 1, t + LEAD)
    if t >= TOK - LEAD and live(n + 2):
        post(n + 2, t + LEAD - TOK)


Q1, Q2, Q3, QT, QE = -12, -9, -8, -6, -4
SCORES, EXP_LAG = -2, 1
O_COPY, O_TURN, O_SQUARE, HEADS, Z_TURN, Z_COPY, WO, YO = 0, 1, 3, 4, 11, 12, 14, 16
GATE, MOB_TANH, X1, LOG_GUESS, LOG_TANH, LOG_FIX, NORM, T2 = 18, 21, 26, 30, 31, 32, 37, 38
T2_TURN, F1, Y1A, Y1B, Y1_TURN, Y1_COPY = 40, 42, 46, 50, (47, 51), (49, 53)
F2, Y2, GATE2, MOB2_TANH, XO, XO_TURN = 50, 58, 60, 63, 68, 71
BIAS = 1
INPUTS = 2
FIRST_INPUTS = 61
FLUSH = (49, 5)
HOLD = 12


def fixed_costs():
    cost = [0.0] * TOK
    for L, c in ((QT, 2), (Z_TURN, 1), (WO, DC), (T2_TURN, 1), (XO_TURN, 1), (O_TURN, 2), (F1, FC), (F2, FC),
                 (Y1_TURN[0], 2), (Y1_TURN[1], 2)):
        for n in range(c):
            cost[(L + n) % TOK] += 2
    for c in range(2):
        for at in FLUSH:
            cost[(LEAD + at + c) % TOK] += 1.3
        cost[(LEAD + FIRST_INPUTS + c) % TOK] += 1
        for k in range(TOK // BLK - 1):
            cost[(LEAD + BLK * k + INPUTS + c) % TOK] += 1
    return cost


def plan(unit_limit, chunk_limit):
    cost, scores, outputs = fixed_costs(), {}, {}
    units, chunks = {}, {}
    for at in range(SCORES, TOK):
        load, scores[at], outputs[at] = cost[at % TOK], [], []
        u = len(units)
        free = u < 2 or units[u - 2] + EXP_LAG < at
        free = free and (u < 8 or KC * (u // 4 - 1) - 1 in chunks)
        if u < H * B and free and load + 2.1 <= unit_limit:
            units[u] = at
            scores[at].append(u)
            load += 2.1
        while len(chunks) < H // QUAD * B * KC and load + 0.9 <= chunk_limit:
            k = len(chunks)
            last = 4 * (k // KC) + 3
            if last not in units or units[last] + EXP_LAG >= at:
                break
            chunks[k] = at
            outputs[at].append(k)
            load += 0.9
        cost[at % TOK] = load
    assert len(chunks) == H // QUAD * B * KC
    return scores, outputs, cost


SCORE_UNITS, OUTPUT_CHUNKS, LOAD = plan(4.7, 3.6)
FIXED = fixed_costs()


def spare(n, t):
    fixed, load = FIXED[(t + LEAD) % TOK], LOAD[(t + LEAD) % TOK]
    ahead = n + (t >= TOK - LEAD) if isinstance(n, int) else 0
    if ahead >= TILES - 1:
        return [3, 3]
    if ahead == TILES - 2:
        return [3, 3] if fixed < 3 else [1]
    return [2] if load < 2.5 else [1] if fixed < 1 else []


EPS = 1e-7
MAXN = float(np.float32(1.0 - 1e-05))
RADIUS = math.atanh(MAXN)
TINY = 1e-30


def _beta(a, b):
    return math.exp(math.lgamma(a) + math.lgamma(b) - math.lgamma(a + b))


BETA_N = _beta(D / 2, 0.5)
BETA_H = _beta(HD / 2, 0.5)
RHO = BETA_H / BETA_N
ONE_BITS = float(127 << 23)
LOG_STEP = 0.5 * math.log(2.0) * 2.0 ** -23
MAGIC = float(0x5F3759DF)


def build(nc, x, cond, w_q, b_q, w_k, b_k, w_v, b_v, w_o, b_o, w_f1, b_f1, w_f2, b_f2, w_ada, b_ada,
          w_x, w_h, b_h, out):
    with ExitStack() as ctx:
        def sb(name, shape, dt=F32):
            return ctx.enter_context(nc.sbuf_tensor(name, shape, dt))

        def sem(name):
            return ctx.enter_context(nc.semaphore(name))

        kT = sb("kT", [96, H, B, S], BF16)
        vals = sb("vals", [P, KC, B, H, HD + 1])
        xp_buf = sb("xp_buf", [P, TILES * D])
        x_all = xp_buf[:].rearrange("p (i d) -> p i d", d=D)
        probs = xp_buf[:].rearrange("p (g j n) -> p g j n", g=2, j=QUAD)
        qf = sb("qf", [P, TILES, D])
        wada_sb = qf[:].rearrange("p i d -> p (i d)")[:, 0:DC * 6 * D].rearrange("p (c n) -> p c n", c=DC)
        wo = sb("wo", [P, DC, D])
        wf1 = sb("wf1", [P, DC, FF])
        wf2 = sb("wf2", [P, FC, D])
        wx = sb("wx", [P, DC, D])
        wh = sb("wh", [P, 2, D])
        bh = sb("bh", [P, D // QUAD])
        mod = sb("mod", [P, 6 * D])
        bo = sb("bo", [P, D])
        bf1 = sb("bf1", [P, FF])
        bf2 = sb("bf2", [P, D])
        bada_row = kT[0:1].rearrange("p h b s -> p (h b s)").bitcast(F32)[:, 0:6 * D]
        condT = sb("condT", [P, DC, B])
        cond_rows = sb("cond_rows", [P, DC, P])
        ident = sb("ident", [P, P])
        ident_bf = sb("ident_bf", [P, P], BF16)
        tiny = sb("tiny", [P, 1])
        ones_row = sb("ones_row", [1, P])
        halves = sb("halves", [P, 2, TILES])
        hist = sb("hist", [P, 2, (TOK + 1) * ROWS])
        xT = sb("xT", [P, DC, P])
        scal = sb("scal", [P, 40, TILES])
        alpha_all = sb("alpha_all", [P, TILES])
        beta_all = sb("beta_all", [P, TILES])
        resid = sb("resid", [P, D])
        work = sb("work", [P, 24 * D])
        stackb = sb("stackb", [P, H, PARTS, HD], BF16)

        def carve(*sizes):
            at, parts = 0, []
            for n in sizes:
                parts.append(work[:, at:at + n])
                at += n
            return parts

        wqkv, t1, t1T, y, ysq0, kf0, junk_p, bqkv = carve(DC * 3 * D, 2 * D, 2 * D, 6 * D, 3 * D, D, D, 3 * D)
        wqkv = wqkv.rearrange("p (c n) -> p c n", c=DC)
        t1 = t1.rearrange("p (e d) -> p e d", e=2)
        t1T = t1T.rearrange("p (e c t) -> p e c t", e=2, c=DC)
        y = y.rearrange("p (e n) -> p e n", e=2)
        bns = y[:, 0, 0:6 * TILES].rearrange("p (i n) -> p i n", n=6)
        hist_flat = hist[:].rearrange("p c n -> p (c n)")
        ysq = (ysq0, hist_flat[:, 0:3 * D])
        kf = (kf0, hist_flat[:, 3 * D:4 * D])
        rest = (resid, hist_flat[:, 4 * D:5 * D])
        stack = (stackb, hist_flat[:, 5 * D:8 * D].bitcast(BF16).rearrange("p (h a d) -> p h a d", h=H, a=PARTS))
        oT, y1, y1T, junk_a, xin, wa, wb, junk_v, x1, xo, aT, oat, wc, xhold = carve(
            2 * D, FF, FF, FF, D, D, D, D, D, D, D, D, D, D)
        y1T = y1T.rearrange("p (c t) -> p c t", c=FC)
        aT = aT.rearrange("p (c t) -> p c t", c=DC)
        qT = sb("qT", [96, H, P], BF16)
        nw = sb("nw", [P, 4, 2 * (3 * H + 3)])
        fac = sb("fac", [P, 2, 3, H])
        fac3 = sb("fac3", [P, 2, 3])
        c1 = sb("c1", [P, 2])
        ss1 = sb("ss1", [P, 2])
        c1t = sb("c1t", [P, 2])
        bn1 = sb("bn1", [P, 6])
        bna = sb("bna", [P, TILES, 2])

        bank = [ctx.enter_context(nc.psum_tensor(f"bank{n}", [P, 512], F32)) for n in range(8)]
        t_bank = bank[0], bank[7]
        y_bank = (bank[1], bank[2]), (bank[5], bank[6])
        k_bank = bank[3:5]
        z_bank = bank[0:2]
        s_bank = bank[2:4]
        a_bank, b_bank = bank[4:6]
        o_bank = bank[6]
        m_bank = bank[7]

        names = """x_in x2_in w_in b_in cond_in gconst gmem ada_done cond_spread mod_done
            st_v st_g st_a st_n bn0_v xn_a t1_g ss_a c1_g t1_pe t1T_a qkv_pe y_v sq_a red_v fac_v f_v q_v v_g o_mem
            k1_a r1_v k2_a k3_v kst_pe kev_a kev_v h0_in
            qr_v q1_a q2_a q3_v qst_pe qev_a qev_v s_pe p_a pv_pe
            o_ev to_pe osq_a of_v zt_v oss_g z_pe zc_a wo_pe yo_v yo2_a co_g w_v w2_a wx_v mob_g bn_v
            th_a th_g th2_a th3_g ln_g xn2_a t2_v t2s_a c2_g t2_pe t2T_a f1_pe y1_v y1s_a c3_g y1_pe y1T_a f2_pe
            y2_v y2s_a c4_g w2_v w22_a w2x_v tm_g tm_a mob2_g xo_v xo_pe xT_a xin_in x_held
            bias_v bits_pe z_pe_step tr_v h_a flush_pe out_v out_dma""".split()
        s = {n: sem(n) for n in names}
        dve_link, pool_link, act_link = sem("dve_link"), sem("pool_link"), sem("act_link")
        block = ctx.enter_context(nc.Block())

        def chain(eng, link_sem):
            count = [0]

            def link(ins):
                count[0] += 1
                ins.then_inc(link_sem, 1)
                eng.wait_ge(link_sem, count[0])

            def then(ins):
                count[0] += 1
                ins.then_inc(link_sem, 1)

            def last():
                if count[0]:
                    eng.wait_ge(link_sem, count[0])

            def restart():
                last()
                eng.sem_clear(link_sem)
                count[0] = 0
            return link, then, last, restart

        def head(e, n, r0=0, r1=P):
            return (y[r0:r1, e, n * D:(n + 1) * D].rearrange("p (h d) -> p h d", h=H),
                    fac[r0:r1, e, n, :].rearrange("p (h o) -> p h o", o=1).broadcast_to([r1 - r0, H, HD]))

        def rows_of(v):
            return v.rearrange("(a n) -> a n", a=1)

        @block.sync
        def _(sp):
            for h, arrived in enumerate((s["x_in"], s["x2_in"])):
                for b in range(B):
                    src = x[b].rearrange("(i t) d -> t i d", t=TOK)
                    sp.dma_start(x_all[b * TOK:(b + 1) * TOK, 8 * h:8 * h + 8, :],
                                 src[:, 8 * h:8 * h + 8, :]).then_inc(arrived, 16)
            for n, w in enumerate((w_q, w_k, w_v)):
                sp.dma_start(wqkv[:, :, n * D:(n + 1) * D],
                             w.rearrange("(c p) n -> p c n", p=P)).then_inc(s["w_in"], 16)
            for dst, w in ((wo, w_o), (wf1, w_f1), (wf2, w_f2), (wx, w_x)):
                sp.dma_start(dst[:], w.rearrange("(c p) n -> p c n", p=P)).then_inc(s["w_in"], 16)
            whv = w_h.rearrange("(j c p) n -> j p c n", c=2, p=32)
            for j in range(QUAD):
                sp.dma_start(wh[32 * j:32 * j + 32, :, :], whv[j]).then_inc(s["w_in"], 16)

            sp.wait_ge(s["gmem"], 2)
            hv = cond.rearrange("b (j c p) -> j c p b", c=2, p=32)
            for j in range(QUAD):
                for c in range(2):
                    sp.dma_start(hist[32 * j:32 * j + 32, c, ROWS * TOK:ROWS * TOK + B], hv[j, c],
                                 allow_slow_non_contiguous=True).then_inc(s["h0_in"], 16)

            def slot(n, t):
                if t == 0 and live(n + 1):
                    wait(sp, s["xo_v"], n + 1)
                    if isinstance(n, int) and n == -1:
                        sp.wait_ge(s["kev_v"], TILES)
                    for b in range(B):
                        sp.dma_start(xin[b * TOK:(b + 1) * TOK, :],
                                     x[b, bass.ds((n + 1) * TOK, TOK), :]).then_inc(s["xin_in"], 16)
                if t == HOLD and live(n):
                    wait(sp, s["out_v"], 2 * n)
                    sp.wait_ge(s["xo_v"], n + 1)
                    sp.dma_start(xhold[:], xo[:]).then_inc(s["x_held"], 16)
                for hh, at in ((1, 9), (0, 53)):
                    m = n - hh
                    if t == at and (not isinstance(n, int) or 0 <= m < TILES):
                        sp.wait_ge(s["out_v"], 2 * m + hh + 1)
                        for b in range(B):
                            q = b * TOK + HALF * hh
                            sp.dma_start(out[b, bass.ds(m * TOK + HALF * hh, HALF), :],
                                         oat[q:q + HALF, :]).then_inc(s["out_dma"], 16)

            walk(sp, slot)
            sp.wait_ge(s["out_dma"], 2 * B * 16 * TILES)

        @block.gpsimd
        def _(pool):
            g = nc.gpsimd
            link, then, last, restart = chain(pool, pool_link)
            g.memset(tiny[:], TINY).then_inc(s["gconst"], 1)
            g.memset(ones_row[:], 1.0).then_inc(s["gconst"], 1)
            g.memset(halves[:, 0, :], 0.5).then_inc(s["gconst"], 1)
            g.memset(halves[:, 1, :], -0.5).then_inc(s["gconst"], 1)
            link(g.memset(ident[:], 0.0))
            g.affine_select(out=ident[:], in_=ident[:], compare_op=ALU.not_equal, fill=1.0, base=0,
                            pattern=[[-1, P]], channel_multiplier=1).then_inc(s["gconst"], 1)
            g.memset(vals[:], 1.0).then_inc(s["gmem"], 1)
            pool.wait_ge(s["gconst"], 5)

            def power(dst, src, half, n):
                link(g.tensor_tensor(dst, src, halves[:, half, 0:n], ALU.pow))

            def sc(k, n=1):
                return scal[:, k, 0:n]

            def log_a(mean, var, n):
                link(g.tensor_tensor(sc(0, n), mean, mean, ALU.mult))
                link(g.tensor_tensor(sc(0, n), sc(0, n), var, ALU.add))
                link(g.tensor_scalar(sc(1, n), sc(0, n), float(D), 0.0, ALU.mult, ALU.max))
                power(sc(2, n), sc(1, n), 0, n)
                link(g.tensor_scalar(sc(2, n), sc(2, n), EPS, None, ALU.max))
                link(g.tensor_scalar(sc(3, n), sc(2, n), MAXN, None, ALU.min))

            def log_b(mean, var, alpha, beta, n):
                link(g.tensor_tensor(sc(9, n), sc(8, n), sc(8, n), ALU.mult))
                link(g.tensor_scalar(sc(10, n), sc(9, n), 0.2, 1.0 / 3.0, ALU.mult, ALU.add))
                link(g.tensor_tensor(sc(10, n), sc(10, n), sc(9, n), ALU.mult))
                link(g.tensor_scalar(sc(10, n), sc(10, n), 1.0, 1.0, ALU.mult, ALU.add))
                link(g.tensor_tensor(sc(10, n), sc(10, n), sc(8, n), ALU.mult))
                link(g.tensor_tensor(sc(10, n), sc(10, n), sc(5, n), ALU.add))
                link(g.tensor_tensor(sc(11, n), sc(10, n), sc(13, n), ALU.mult))
                link(g.tensor_tensor(sc(12, n), sc(11, n), sc(11, n), ALU.mult))
                link(g.tensor_tensor(sc(12, n), sc(12, n), var, ALU.mult))
                link(g.tensor_scalar(sc(12, n), sc(12, n), 1e-6, 0.0, ALU.add, ALU.max))
                power(sc(14, n), sc(12, n), 1, n)
                link(g.tensor_tensor(alpha, sc(14, n), sc(11, n), ALU.mult))
                link(g.tensor_tensor(sc(15, n), alpha, mean, ALU.mult))
                return g.tensor_scalar(beta, sc(15, n), -1.0, 0.0, ALU.mult, ALU.add)

            def clip(dst, src, tmp, factor=RADIUS):
                link(g.tensor_tensor(tmp, src, tiny[:], ALU.add))
                power(tmp, tmp, 1, 1)
                return g.tensor_scalar(dst, tmp, factor, 1.0, ALU.mult, ALU.min)

            pool.wait_ge(s["st_v"], 1)
            log_a(bna[:, :, 0], bna[:, :, 1], TILES)
            g.tensor_copy(sc(16, TILES), sc(3, TILES)).then_inc(s["st_g"], 1)
            pool.wait_ge(s["st_n"], 2)
            log_b(bna[:, :, 0], bna[:, :, 1], alpha_all[:], beta_all[:], TILES).then_inc(s["st_g"], 1)

            def modulate(m):
                for e in range(2):
                    pool.wait_ge(s["xn_a"], 2 * m + e + 1)
                    link(g.tensor_tensor(t1[:, e, :], t1[:, e, :], mod[:, D:2 * D], ALU.mult))
                    g.tensor_tensor(t1[:, e, :], t1[:, e, :], mod[:, 0:D], ALU.add).then_inc(s["t1_g"], 1)

            def clips(m):
                for e in range(2):
                    pool.wait_ge(s["ss_a"], 2 * m + e + 1)
                    wait(pool, s["y_v"], 2 * m + e - 1)
                    clip(c1[:, e:e + 1], ss1[:, e:e + 1], c1t[:, e:e + 1]).then_inc(s["c1_g"], 1)

            def prepare(m, left):
                if left:
                    clips(m + 1)
                restart()
                pool.wait_ge(s["fac_v"], m + 1)
                for e in range(2):
                    for b in range(B):
                        yv, fv = head(e, 2, b * TOK, (b + 1) * TOK)
                        vm = g.tensor_tensor(vals[e * TOK:(e + 1) * TOK, bass.ds(m, 1), b, :, 0:HD]
                                             .rearrange("p a h d -> p (a h) d"), yv, fv, ALU.mult)
                        if b == 0:
                            link(vm)
                    vm.then_inc(s["v_g"], 1)
                    pool.wait_ge(s["v_g"], 2 * m + e + 1)
                if left == 2:
                    modulate(m + 2)

            pool.wait_ge(s["mod_done"], 5)
            modulate(0)
            clips(0)
            modulate(1)
            restart()
            pairs(pool, prepare)
            restart()
            pool.wait_ge(s["kev_v"], TILES)
            g.memset(hist[:], 0.0).then_inc(s["gmem"], 1)

            def mobius(n_tanh, ss_w, dot, ss_x, p_out, q_out, tm_g, tm_a, i1):
                power(sc(20), ss_w, 0, 1)
                link(g.tensor_scalar(sc(20), sc(20), EPS, None, ALU.max))
                power(sc(22), sc(20), 1, 1)
                g.tensor_tensor(sc(22), sc(22), sc(22), ALU.mult).then_inc(tm_g, 1)
                pool.wait_ge(tm_a, i1)
                link(g.tensor_tensor(sc(23), sc(21), sc(22), ALU.mult))
                link(g.tensor_tensor(sc(24), sc(23), sc(23), ALU.mult))
                link(g.tensor_tensor(sc(24), sc(24), ss_w, ALU.mult))
                link(g.tensor_tensor(sc(25), sc(23), dot, ALU.mult))
                link(g.tensor_scalar(sc(26), sc(25), 2.0, 1.0, ALU.mult, ALU.add))
                link(g.tensor_tensor(sc(27), sc(26), sc(24), ALU.add))
                link(g.tensor_tensor(sc(28), ss_x, sc(24), ALU.mult))
                link(g.tensor_tensor(sc(28), sc(28), sc(26), ALU.add))
                link(g.tensor_scalar(sc(28), sc(28), EPS, None, ALU.max))
                power(sc(29), sc(28), 1, 1)
                link(g.tensor_tensor(sc(29), sc(29), sc(29), ALU.mult))
                link(g.tensor_tensor(p_out, sc(27), sc(29), ALU.mult))
                link(g.tensor_scalar(sc(30), ss_x, -1.0, 1.0, ALU.mult, ALU.add))
                link(g.tensor_tensor(sc(30), sc(30), sc(29), ALU.mult))
                return g.tensor_tensor(q_out, sc(30), sc(23), ALU.mult)

            def post(i, L):
                i1 = i + 1
                if L == HEADS:
                    pool.wait_ge(s["of_v"], i1)
                    clip(scal[:, 31, 1:2], scal[:, 31, 0:1], scal[:, 31, 2:3]).then_inc(s["oss_g"], 1)
                if L == YO:
                    pool.wait_ge(s["yo2_a"], i1)
                    clip(scal[:, 32, 1:2], scal[:, 32, 0:1], scal[:, 32, 2:3]).then_inc(s["co_g"], 1)
                if L == GATE:
                    pool.wait_ge(s["w2_a"], i1)
                    pool.wait_ge(s["wx_v"], i1)
                    mobius(sc(21), scal[:, 33, 0:1], scal[:, 33, 1:2], scal[:, 33, 2:3],
                           scal[:, 34, 0:1], scal[:, 34, 1:2], s["tm_g"], s["tm_a"], 2 * i + 1)\
                        .then_inc(s["mob_g"], 1)
                if L == X1:
                    pool.wait_ge(s["bn_v"], i1)
                    log_a(scal[:, 35, 0:1], scal[:, 35, 1:2], 1)
                    g.tensor_copy(sc(16), sc(3)).then_inc(s["th_g"], 1)
                if L == LOG_FIX + 1:
                    pool.wait_ge(s["th3_g"], i1)
                    log_b(scal[:, 35, 0:1], scal[:, 35, 1:2], scal[:, 36, 0:1], scal[:, 36, 1:2], 1)\
                        .then_inc(s["ln_g"], 1)
                if L == T2_TURN:
                    pool.wait_ge(s["t2s_a"], i1)
                    clip(scal[:, 37, 1:2], scal[:, 37, 0:1], scal[:, 37, 2:3]).then_inc(s["c2_g"], 1)
                if L == Y1B + 1:
                    pool.wait_ge(s["y1s_a"], 2 * i + 2)
                    link(g.tensor_tensor(scal[:, 38, 0:1], scal[:, 38, 0:1], scal[:, 38, 3:4], ALU.add))
                    clip(scal[:, 38, 1:2], scal[:, 38, 0:1], scal[:, 38, 2:3]).then_inc(s["c3_g"], 1)
                if L == Y2:
                    pool.wait_ge(s["y2s_a"], i1)
                    clip(scal[:, 39, 1:2], scal[:, 39, 0:1], scal[:, 39, 2:3]).then_inc(s["c4_g"], 1)
                if L == GATE2:
                    pool.wait_ge(s["w22_a"], i1)
                    pool.wait_ge(s["w2x_v"], i1)
                    mobius(sc(21), scal[:, 33, 3:4], scal[:, 33, 4:5], sc(1),
                           scal[:, 34, 2:3], scal[:, 34, 3:4], s["tm_g"], s["tm_a"], 2 * i + 2)\
                        .then_inc(s["mob2_g"], 1)

            def slot(n, t):
                parts(n, t, lambda i, l: None, post)
                if t == TOK - 1:
                    restart()

            walk(pool, slot)

        @block.scalar
        def _(act):
            a = nc.scalar
            for c in range(DC):
                act.dma_start(wada_sb[:, c, :], w_ada[c * P:(c + 1) * P, :]).then_inc(s["cond_in"], 16)
            for c in range(DC):
                act.dma_start(condT[:, c, :], cond[:, c * P:(c + 1) * P].rearrange("b p -> p b"),
                              allow_slow_non_contiguous=True).then_inc(s["cond_in"], 16)
            act.dma_start(bada_row[:], rows_of(b_ada)).then_inc(s["cond_in"], 16)
            for n, bvec in enumerate((b_q, b_k, b_v)):
                act.dma_start(bqkv[:, n * D:(n + 1) * D], rows_of(bvec).broadcast_to([P, D])).then_inc(s["b_in"], 16)
            for dst, bvec, n in ((bo, b_o, D), (bf1, b_f1, FF), (bf2, b_f2, D)):
                act.dma_start(dst[:], rows_of(bvec).broadcast_to([P, n])).then_inc(s["b_in"], 16)
            for j in range(QUAD):
                act.dma_start(bh[32 * j:32 * j + 32, :], rows_of(b_h[64 * j:64 * j + 64]).broadcast_to([32, 64]))\
                    .then_inc(s["b_in"], 16)
            act.wait_ge(s["st_v"], 2)
            a.activation(scal[:, 6, :], scal[:, 5, :], ACT.Tanh).then_inc(s["st_a"], 1)

            def normal(m):
                for e in range(2):
                    wait(act, s["t1_pe"], 2 * m + e - 1)
                    wait(act, s["ss_a"], 2 * m + e - 1)
                    a.activation(t1[:, e, :], x_all[:, bass.ds(2 * m + e, 1), :].rearrange("p a d -> p (a d)"),
                                 ACT.Identity, bias=beta_all[:, bass.ds(2 * m + e, 1)],
                                 scale=alpha_all[:, bass.ds(2 * m + e, 1)]).then_inc(s["xn_a"], 1)

            def turned(m):
                for e in range(2):
                    act.wait_ge(s["t1_g"], 2 * m + e + 1)
                    wait(act, s["c1_g"], 2 * m + e - 1)
                    wait(act, s["ss_a"], 2 * m + e)
                    a.activation(junk_p[:], t1[:, e, :], ACT.Square, accum_out=ss1[:, e:e + 1]).then_inc(s["ss_a"], 1)
                    act.wait_ge(s["t1_pe"], 2 * m + e + 1)
                    wait(act, s["qkv_pe"], 2 * m + e - 1)
                    a.activation(t1T[:, e, :, :], t_bank[e][:, 0:D].rearrange("p (c t) -> p c t", c=DC),
                                 ACT.Copy).then_inc(s["t1T_a"], 1)

            def squares(m):
                for e in range(2):
                    act.wait_ge(s["y_v"], 2 * m + e + 1)
                    wait(act, s["red_v"], 2 * m + e - 1)
                    a.activation(ysq[e][:], y[:, e, :], ACT.Square).then_inc(s["sq_a"], 1)

            def prepare(m, left):
                if left:
                    turned(m + 1)
                for e in range(2):
                    act.wait_ge(s["f_v"], 2 * m + e + 1)
                    k_h = kf[e][:].rearrange("p (h o d) -> p h o d", h=H, o=1)
                    a.activation(stack[e][:, :, 0:3, :], k_h.broadcast_to([P, H, 3, HD]), ACT.Copy)\
                        .then_inc(s["k1_a"], 1)
                for e in range(2):
                    act.wait_ge(s["r1_v"], 2 * m + e + 1)
                    r_h = rest[e][:].rearrange("p (h o d) -> p h o d", h=H, o=1)
                    a.activation(stack[e][:, :, 3:5, :], r_h.broadcast_to([P, H, 2, HD]), ACT.Copy)\
                        .then_inc(s["k2_a"], 1)
                if left == 2:
                    normal(m + 2)
                for e in range(2):
                    act.wait_ge(s["kst_pe"], 4 * m + 2 * e + 1)
                    a.activation(kT[:, 0:8, :, bass.ds((2 * m + e) * TOK, TOK)],
                                 k_bank[0][:].bitcast(BF16)[0:96, :].rearrange("p (h b t) -> p h b t", h=8, b=B),
                                 ACT.Copy).then_inc(s["kev_a"], 1)
                    if left and e == 0:
                        squares(m + 1)

            act.wait_ge(s["st_g"], 2)
            normal(0)
            turned(0)
            normal(1)
            squares(0)
            pairs(act, prepare)
            def att(i, l):
                i1 = i + 1
                if l == Q1:
                    q_h = qf[:, bass.ds(i, 1), :].rearrange("p a (h o d) -> p (a h) o d", h=H, o=1)
                    wait(act, s["qst_pe"], 2 * i)
                    a.activation(stackb[:, :, 0:4:3, :], q_h.broadcast_to([P, H, 2, HD]), ACT.Copy)
                    a.activation(stackb[:, :, 5:6, :], q_h, ACT.Copy).then_inc(s["q1_a"], 1)
                if l == Q2:
                    act.wait_ge(s["qr_v"], i1)
                    r_h = resid[:].rearrange("p (h o d) -> p h o d", h=H, o=1)
                    a.activation(stackb[:, :, 1:5:3, :], r_h.broadcast_to([P, H, 2, HD]), ACT.Copy)\
                        .then_inc(s["q2_a"], 1)
                if l in (QE, QE + 1):
                    r = 4 * (l - QE)
                    if l == QE:
                        act.wait_ge(s["qst_pe"], 2 * i + 1)
                    a.activation(qT[:, r:r + 4, :],
                                 s_bank[0][:].bitcast(BF16)[0:96, r * P:(r + 4) * P].rearrange("p (h t) -> p h t", h=4),
                                 ACT.Copy).then_inc(s["qev_a"], 1)
                for u in SCORE_UNITS.get(l - EXP_LAG, ()):
                    gb, j = u // 4, u % 4
                    act.wait_ge(s["s_pe"], 32 * i + u + 1)
                    if j == 0:
                        wait(act, s["pv_pe"], 8 * i + gb - 1)
                    a.activation(probs[:, gb % 2, j, :], s_bank[u % 2][:, :], ACT.Exp).then_inc(s["p_a"], 1)

            def post(i, L):
                i1 = i + 1
                if L == O_COPY:
                    act.wait_ge(s["pv_pe"], 8 * i + 8)
                    a.activation(oT[:], o_bank[:, :], ACT.Copy).then_inc(s["o_ev"], 1)
                if L == O_SQUARE:
                    act.wait_ge(s["to_pe"], i1)
                    to = a_bank[:].rearrange("p (h r) -> p h r", h=H)
                    a.activation(junk_a[:, 0:D].rearrange("p (h d) -> p h d", h=H), to[:, :, 0:HD], ACT.Square)\
                        .then_inc(s["osq_a"], 1)
                if L == Z_COPY:
                    act.wait_ge(s["z_pe"], i1)
                    a.activation(aT[:], a_bank[:, 0:D].rearrange("p (c t) -> p c t", c=DC), ACT.Copy)\
                        .then_inc(s["zc_a"], 1)
                if L == WO:
                    act.wait_ge(s["xin_in"], 32 * i + 32)
                    a.activation(junk_a[:, 256:512], xin[:], ACT.Square, accum_out=scal[:, 33, 2:3])
                if L == YO:
                    act.wait_ge(s["yo_v"], i1)
                    a.activation(junk_a[:, 512:768], wa[:], ACT.Square, accum_out=scal[:, 32, 0:1])\
                        .then_inc(s["yo2_a"], 1)
                if L == GATE:
                    act.wait_ge(s["w_v"], i1)
                    a.activation(junk_a[:, 768:1024], wb[:], ACT.Square, accum_out=scal[:, 33, 0:1])\
                        .then_inc(s["w2_a"], 1)
                if L == MOB_TANH:
                    act.wait_ge(s["tm_g"], 2 * i + 1)
                    a.activation(scal[:, 21, 0:1], scal[:, 20, 0:1], ACT.Tanh).then_inc(s["tm_a"], 1)
                if L == LOG_TANH:
                    act.wait_ge(s["th_a"], i1)
                    a.activation(scal[:, 6, 0:1], scal[:, 5, 0:1], ACT.Tanh).then_inc(s["th2_a"], 1)
                if L == NORM:
                    act.wait_ge(s["ln_g"], i1)
                    a.activation(wa[:], x1[:], ACT.Identity, bias=scal[:, 36, 1:2], scale=scal[:, 36, 0:1])\
                        .then_inc(s["xn2_a"], 1)
                if L == T2_TURN:
                    act.wait_ge(s["t2_v"], i1)
                    a.activation(junk_a[:, 0:256], wb[:], ACT.Square, accum_out=scal[:, 37, 0:1])\
                        .then_inc(s["t2s_a"], 1)
                if L == T2_TURN + 1:
                    act.wait_ge(s["t2_pe"], i1)
                    a.activation(aT[:], a_bank[:, 0:D].rearrange("p (c t) -> p c t", c=DC), ACT.Copy)\
                        .then_inc(s["t2T_a"], 1)
                if L == Y1A + 1:
                    act.wait_ge(s["y1_v"], 2 * i + 1)
                    a.activation(junk_a[:, 0:512], y1[:, 0:512], ACT.Square, accum_out=scal[:, 38, 0:1])\
                        .then_inc(s["y1s_a"], 1)
                if L == Y1B + 1:
                    act.wait_ge(s["y1_v"], 2 * i + 2)
                    a.activation(junk_a[:, 512:1024], y1[:, 512:1024], ACT.Square, accum_out=scal[:, 38, 3:4])\
                        .then_inc(s["y1s_a"], 1)
                for half, at, bk in ((0, Y1_COPY[0], a_bank), (1, Y1_COPY[1], b_bank)):
                    if L == at:
                        act.wait_ge(s["y1_pe"], 2 * i + half + 1)
                        a.activation(y1T[:, 4 * half:4 * half + 4, :], bk[:].rearrange("p (c t) -> p c t", c=4),
                                     ACT.Copy).then_inc(s["y1T_a"], 1)
                if L == Y2:
                    act.wait_ge(s["y2_v"], i1)
                    a.activation(junk_a[:, 256:512], wa[:], ACT.Square, accum_out=scal[:, 39, 0:1])\
                        .then_inc(s["y2s_a"], 1)
                if L == GATE2:
                    act.wait_ge(s["w2_v"], i1)
                    a.activation(junk_a[:, 512:768], wb[:], ACT.Square, accum_out=scal[:, 33, 3:4])\
                        .then_inc(s["w22_a"], 1)
                if L == MOB2_TANH:
                    act.wait_ge(s["tm_g"], 2 * i + 2)
                    a.activation(scal[:, 21, 0:1], scal[:, 20, 0:1], ACT.Tanh).then_inc(s["tm_a"], 1)
                if L == XO_TURN + 1:
                    act.wait_ge(s["xo_pe"], i1)
                    a.activation(xT[:].rearrange("p c (t b) -> p c b t", b=B),
                                 m_bank[:, 0:D].rearrange("p (c b t) -> p c b t", c=DC, b=B), ACT.Copy)\
                        .then_inc(s["xT_a"], 1)

            def rnn_step(n, t):
                m = t % BLK
                z = z_bank[(t // BLK) % 2]
                act.wait_ge(s["tr_v"], n * TOK + t + 1)
                a.activation(hist[:, :, ROWS * (t + 1):ROWS * (t + 1) + B],
                             z[:, 64:128].rearrange("p (c r) -> p c r", c=2)[:, :, B * m:B * m + B],
                             ACT.Tanh).then_inc(s["h_a"], 1)

            def slot(n, t):
                if isinstance(n, int) and (n, t) == (-1, TOK - 1):
                    act.wait_ge(s["h0_in"], 16 * 2 * QUAD)
                    act.nop().then_inc(s["h_a"], 1)
                if live(n):
                    rnn_step(n, t)
                parts(n, t, att, post)

            act.wait_ge(s["kst_pe"], 2 * TILES)
            walk(act, slot)

        @block.vector
        def _(dve):
            v = nc.vector
            link, then, last, restart = chain(dve, dve_link)
            restart()
            dve.wait_ge(s["gconst"], 5)
            v.tensor_copy(ident_bf[:], ident[:]).then_inc(s["cond_spread"], 1)
            for i in range(TILES):
                if i == 0:
                    dve.wait_ge(s["x_in"], 32)
                if i == 8:
                    dve.wait_ge(s["x2_in"], 32)
                v.bn_stats(bns[:, i, :], x_all[:, i, :]).then_inc(s["bn0_v"], 1)
            dve.wait_ge(s["cond_in"], 80)
            for c in range(DC):
                for b in range(B):
                    v.tensor_scalar(cond_rows[:, c, b * TOK:(b + 1) * TOK], ident[:, 0:TOK], 0.0, condT[:, c, b:b + 1],
                                    ALU.mult, ALU.add).then_inc(s["cond_spread"], 1)
            dve.wait_ge(s["bn0_v"], TILES)
            for i in range(TILES):
                ins = v.bn_aggr(bna[:, i, :], bns[:, i, :])
            ins.then_inc(s["st_v"], 1)

            def sc(k, n=1):
                return scal[:, k, 0:n]

            def guess(n):
                link(v.tensor_scalar(sc(4, n), sc(16, n), -1.0, 1.0, ALU.mult, ALU.add))
                link(v.reciprocal(sc(4, n), sc(4, n)))
                link(v.scalar_tensor_tensor(sc(4, n), sc(16, n), 1.0, sc(4, n), ALU.add, ALU.mult))
                return v.tensor_scalar(sc(5, n), sc(4, n).bitcast(I32), ONE_BITS, LOG_STEP, ALU.subtract, ALU.mult)

            def correct(n, part):
                if part == 0:
                    link(v.tensor_tensor(sc(7, n), sc(16, n), sc(6, n), ALU.mult))
                    link(v.tensor_scalar(sc(7, n), sc(7, n), -1.0, 1.0, ALU.mult, ALU.add))
                    link(v.reciprocal(sc(7, n), sc(7, n)))
                    return None
                link(v.tensor_tensor(sc(8, n), sc(16, n), sc(6, n), ALU.subtract))
                link(v.tensor_tensor(sc(8, n), sc(8, n), sc(7, n), ALU.mult))
                return v.reciprocal(sc(13, n), sc(2, n))

            dve.wait_ge(s["st_g"], 1)
            guess(TILES).then_inc(s["st_v"], 1)
            dve.wait_ge(s["st_a"], 1)
            correct(TILES, 0)
            correct(TILES, 1).then_inc(s["st_n"], 2)

            dve.wait_ge(s["ada_done"], 1)
            for n in range(3):
                v.tensor_copy(mod[:, n * 512:(n + 1) * 512], bank[n][:, :]).then_inc(s["mod_done"], 1)
            dve.wait_ge(s["mod_done"], 3)
            for n in (1, 4):
                v.tensor_scalar(mod[:, n * D:(n + 1) * D], mod[:, n * D:(n + 1) * D], 1.0, None, ALU.add)\
                    .then_inc(s["mod_done"], 1)
            dve.wait_ge(s["mod_done"], 5)

            def rsqrt(y_, x_, t_, bits):
                link(v.tensor_scalar(bits, x_.bitcast(I32), 1, None, ALU.logical_shift_right))
                link(v.tensor_scalar(y_.bitcast(I32), bits, -1.0, MAGIC, ALU.mult, ALU.add))
                for _ in range(3):
                    link(v.scalar_tensor_tensor(t_, y_, -0.5, y_, ALU.mult, ALU.mult))
                    link(v.tensor_tensor(t_, t_, x_, ALU.mult))
                    link(v.scalar_tensor_tensor(y_, t_, 1.5, y_, ALU.add, ALU.mult))

            N = 3 * H

            def scaled(m, e):
                dve.wait_ge(s["c1_g"], 2 * m + e + 1)
                dve.wait_ge(s["qkv_pe"], 2 * m + e + 1)
                wait(dve, s["v_g"], 2 * m + e - 1)
                wait(dve, s["q_v"], 2 * m + e - 1)
                v.scalar_tensor_tensor(y[:, e, 0:512], y_bank[e][0][:, :], c1[:, e:e + 1], bqkv[:, 0:512],
                                       ALU.mult, ALU.add)
                v.scalar_tensor_tensor(y[:, e, 512:768], y_bank[e][1][:, 0:D], c1[:, e:e + 1], bqkv[:, 512:768],
                                       ALU.mult, ALU.add).then_inc(s["y_v"], 1)

            def kev(m, e):
                dve.wait_ge(s["kst_pe"], 4 * m + 2 * e + 2)
                v.tensor_copy(kT[:, 8:16, :, bass.ds((2 * m + e) * TOK, TOK)],
                              k_bank[1][:].bitcast(BF16)[0:96, :].rearrange("p (h b t) -> p h b t", h=8, b=B))\
                    .then_inc(s["kev_v"], 1)

            def prepare(m, left):
                n4 = nw[:, 0, :].rearrange("p (e n) -> p e n", e=2)
                for e in range(2):
                    dve.wait_ge(s["sq_a"], 2 * m + e + 1)
                    v.tensor_reduce(n4[:, e, 0:N], ysq[e][:].rearrange("p (h d) -> p h d", d=HD), AX_X, ALU.add)\
                        .then_inc(s["red_v"], 1)
                dve.wait_ge(s["red_v"], 2 * m + 2)
                for e in range(2):
                    ins = v.tensor_reduce(n4[:, e, N:N + 3], n4[:, e, 0:N].rearrange("p (n h) -> p n h", n=3),
                                          AX_X, ALU.add)
                link(ins)
                link(v.tensor_scalar(nw[:, 0, :], nw[:, 0, :], TINY, None, ALU.max))
                rsqrt(nw[:, 1, :], nw[:, 0, :], nw[:, 2, :], nw[:, 3, :].bitcast(I32))
                r4 = nw[:, 1, :].rearrange("p (e n) -> p e n", e=2)
                link(v.tensor_scalar(fac3[:], r4[:, :, N:N + 3], RHO * RADIUS, RHO, ALU.mult, ALU.min))
                for e in range(2):
                    f3 = fac3[:, e, :].rearrange("p (n o) -> p n o", o=1).broadcast_to([P, 3, H])
                    ins = v.scalar_tensor_tensor(fac[:, e, :, :], r4[:, e, 0:N].rearrange("p (n h) -> p n h", n=3),
                                                 RADIUS, f3, ALU.mult, ALU.min)
                ins.then_inc(s["fac_v"], 1)
                dve.wait_ge(s["fac_v"], m + 1)
                for e in range(2):
                    yk, fk = head(e, 1)
                    v.tensor_tensor(kf[e][:].rearrange("p (h d) -> p h d", h=H), yk, fk, ALU.mult).then_inc(s["f_v"], 1)
                link(v.tensor_scalar(fac[:, :, 0, :], fac[:, :, 0, :], 1.0 / math.sqrt(HD), None, ALU.mult))
                for e in range(2):
                    yq, fq = head(e, 0)
                    v.tensor_tensor(qf[:, bass.ds(2 * m + e, 1), :].rearrange("p a (h d) -> p (a h) d", h=H),
                                    yq, fq, ALU.mult).then_inc(s["q_v"], 1)
                for e in range(2):
                    dve.wait_ge(s["k1_a"], 2 * m + e + 1)
                    v.tensor_tensor(rest[e][:].rearrange("p (h d) -> p h d", h=H),
                                    kf[e][:].rearrange("p (h d) -> p h d", h=H),
                                    stack[e][:, :, 0, :], ALU.subtract).then_inc(s["r1_v"], 1)
                for e in range(2):
                    dve.wait_ge(s["k2_a"], 2 * m + e + 1)
                    v.tensor_tensor(stack[e][:, :, 5, :], rest[e][:].rearrange("p (h d) -> p h d", h=H),
                                    stack[e][:, :, 3, :], ALU.subtract).then_inc(s["k3_v"], 1)
                if left:
                    scaled(m + 1, 0)
                kev(m, 0)
                if left:
                    scaled(m + 1, 1)
                kev(m, 1)
                restart()

            dve.wait_ge(s["b_in"], 16 * 10)
            scaled(0, 0)
            scaled(0, 1)
            restart()
            pairs(dve, prepare)
            v.memset(o_bank[:, :], 0.0).then_inc(s["o_mem"], 1)

            def att(i, l):
                i1 = i + 1
                r = resid[:].rearrange("p (h d) -> p h d", h=H)
                if l == Q1 + 1:
                    dve.wait_ge(s["q1_a"], i1)
                    v.tensor_tensor(r, qf[:, bass.ds(i, 1), :].rearrange("p a (h d) -> p (a h) d", h=H),
                                    stackb[:, :, 0, :], ALU.subtract).then_inc(s["qr_v"], 1)
                if l == Q3:
                    dve.wait_ge(s["q2_a"], i1)
                    v.tensor_tensor(stackb[:, :, 2, :], r, stackb[:, :, 1, :], ALU.subtract).then_inc(s["q3_v"], 1)
                if l in (QE + 1, QE + 2):
                    o = 4 * (l - QE - 1)
                    if l == QE + 1:
                        dve.wait_ge(s["qst_pe"], 2 * i + 2)
                    v.tensor_copy(qT[:, 8 + o:12 + o, :], s_bank[1][:].bitcast(BF16)[0:96, o * P:(o + 4) * P]
                                  .rearrange("p (h t) -> p h t", h=4)).then_inc(s["qev_v"], 1)

            def heads(i, part):
                to = a_bank[:].rearrange("p (h r) -> p h r", h=H)
                rec, ssq = fac[:, 0, 0, :], fac[:, 0, 1, :]
                n2, r_, t_, bits = nw[:, 0, 0:H], nw[:, 1, 0:H], nw[:, 2, 0:H], nw[:, 3, 0:H].bitcast(I32)
                if part == 0:
                    dve.wait_ge(s["osq_a"], i + 1)
                    then(v.reciprocal(rec, to[:, :, HD]))
                    then(v.tensor_reduce(ssq, junk_a[:, 0:D].rearrange("p (h d) -> p h d", h=H), AX_X, ALU.add))
                    last()
                    then(v.scalar_tensor_tensor(n2, ssq, TINY, rec, ALU.add, ALU.mult))
                if part == 1:
                    last()
                    then(v.scalar_tensor_tensor(n2, n2, TINY, rec, ALU.add, ALU.mult))
                    last()
                    then(v.tensor_scalar(bits, n2.bitcast(I32), 1, None, ALU.logical_shift_right))
                    last()
                    then(v.tensor_scalar(r_.bitcast(I32), bits, -1.0, MAGIC, ALU.mult, ALU.add))
                if part in (2, 3, 4):
                    last()
                    then(v.scalar_tensor_tensor(t_, r_, -0.5, r_, ALU.mult, ALU.mult))
                    last()
                    then(v.tensor_tensor(t_, t_, n2, ALU.mult))
                    last()
                    then(v.scalar_tensor_tensor(r_, t_, 1.5, r_, ALU.add, ALU.mult))
                if part == 5:
                    last()
                    then(v.tensor_scalar(r_, r_, RADIUS / RHO, 1.0 / RHO, ALU.mult, ALU.min))
                    last()
                    then(v.tensor_tensor(t_, r_, r_, ALU.mult))
                    then(v.tensor_tensor(ssq, r_, rec, ALU.mult))
                    last()
                    then(v.tensor_tensor(t_, t_, n2, ALU.mult))
                    last()
                    v.tensor_reduce(scal[:, 31, 0:1], t_, AX_X, ALU.add).then_inc(s["of_v"], 1)
                if part == 6:
                    v.tensor_tensor(wc[:].rearrange("p (h d) -> p h d", h=H), to[:, :, 0:HD],
                                    ssq.rearrange("p (h o) -> p h o", o=1).broadcast_to([P, H, HD]),
                                    ALU.mult).then_inc(s["zt_v"], 1)

            def post(i, L):
                i1 = i + 1
                if HEADS <= L < HEADS + 7:
                    heads(i, L - HEADS)
                if L == YO:
                    dve.wait_ge(s["wo_pe"], i1)
                    dve.wait_ge(s["oss_g"], i1)
                    v.scalar_tensor_tensor(wa[:], b_bank[:, 0:D], scal[:, 31, 1:2], bo[:], ALU.mult, ALU.add)\
                        .then_inc(s["yo_v"], 1)
                if L == GATE:
                    dve.wait_ge(s["co_g"], i1)
                    v.scalar_tensor_tensor(wb[:], wa[:], scal[:, 32, 1:2], mod[:, 2 * D:3 * D], ALU.mult, ALU.mult)\
                        .then_inc(s["w_v"], 1)
                    dve.wait_ge(s["w_v"], i1)
                    dve.wait_ge(s["xin_in"], 32 * i + 32)
                    v.tensor_tensor_reduce(junk_v[:], wb[:], xin[:], 1.0, 0.0, ALU.mult, ALU.add, scal[:, 33, 1:2])\
                        .then_inc(s["wx_v"], 1)
                if L == X1:
                    dve.wait_ge(s["mob_g"], i1)
                    then(v.tensor_scalar(wb[:], wb[:], scal[:, 34, 1:2], None, ALU.mult))
                    last()
                    then(v.scalar_tensor_tensor(x1[:], xin[:], scal[:, 34, 0:1], wb[:], ALU.mult, ALU.add))
                if L == X1 + 1:
                    last()
                    then(v.bn_stats(bn1[:], x1[:]))
                    last()
                    v.bn_aggr(scal[:, 35, 0:2], bn1[:]).then_inc(s["bn_v"], 1)
                if L == LOG_GUESS:
                    dve.wait_ge(s["th_g"], i1)
                    guess(1).then_inc(s["th_a"], 1)
                if L == LOG_FIX:
                    dve.wait_ge(s["th2_a"], i1)
                    correct(1, 0)
                if L == LOG_FIX + 1:
                    correct(1, 1).then_inc(s["th3_g"], 1)
                if L == T2:
                    dve.wait_ge(s["xn2_a"], i1)
                    then(v.tensor_tensor(wb[:], wa[:], mod[:, 4 * D:5 * D], ALU.mult))
                if L == T2 + 1:
                    last()
                    v.tensor_tensor(wb[:], wb[:], mod[:, 3 * D:4 * D], ALU.add).then_inc(s["t2_v"], 1)
                for half, at, bk in ((0, Y1A, a_bank), (1, Y1B, b_bank)):
                    if L == at:
                        dve.wait_ge(s["c2_g"], i1)
                        dve.wait_ge(s["f1_pe"], 2 * i + half + 1)
                        o = 512 * half
                        v.scalar_tensor_tensor(y1[:, o:o + 512], bk[:, :], scal[:, 37, 1:2], bf1[:, o:o + 512],
                                               ALU.mult, ALU.add).then_inc(s["y1_v"], 1)
                if L == Y2:
                    dve.wait_ge(s["c3_g"], i1)
                    dve.wait_ge(s["f2_pe"], i1)
                    v.scalar_tensor_tensor(wa[:], m_bank[:, 256:512], scal[:, 38, 1:2], bf2[:], ALU.mult, ALU.add)\
                        .then_inc(s["y2_v"], 1)
                if L == GATE2:
                    dve.wait_ge(s["c4_g"], i1)
                    v.scalar_tensor_tensor(wb[:], wa[:], scal[:, 39, 1:2], mod[:, 5 * D:6 * D], ALU.mult, ALU.mult)\
                        .then_inc(s["w2_v"], 1)
                    dve.wait_ge(s["w2_v"], i1)
                    v.tensor_tensor_reduce(junk_v[:], wb[:], x1[:], 1.0, 0.0, ALU.mult, ALU.add, scal[:, 33, 4:5])\
                        .then_inc(s["w2x_v"], 1)
                if L == XO:
                    dve.wait_ge(s["mob2_g"], i1)
                    wait(dve, s["x_held"], 16 * i)
                    then(v.tensor_scalar(wb[:], wb[:], scal[:, 34, 3:4], None, ALU.mult))
                if L == XO + 1:
                    last()
                    then(v.scalar_tensor_tensor(wb[:], x1[:], scal[:, 34, 2:3], wb[:], ALU.mult, ALU.add))
                if L == XO + 2:
                    last()
                    v.tensor_tensor(xo[:], wb[:], xin[:], ALU.add).then_inc(s["xo_v"], 1)

            def rnn_step(n, t):
                z = z_bank[(t // BLK) % 2]
                dve.wait_ge(s["z_pe_step"], n * TOK + t + 1)
                v.transpose(z[:, 64:128], z[:, 0:64]).then_inc(s["tr_v"], 1)

            def store(n, hh):
                dve.wait_ge(s["flush_pe"], 2 * n + hh + 1)
                wait(dve, s["out_dma"], 32 * (2 * n + hh - 1))
                dve.wait_ge(s["x_held"], 16 * (n + 1))
                for b in range(B):
                    q = b * TOK + HALF * hh
                    ins = v.tensor_tensor(oat[q:q + HALF, :], m_bank[q:q + HALF, 0:D], xhold[q:q + HALF, :], ALU.add)
                ins.then_inc(s["out_v"], 1)

            def bias(n, k):
                if isinstance(n, int) and n == 0 and k < 2:
                    dve.wait_ge(s["bits_pe"], 2)
                else:
                    dve.wait_ge(s["h_a"], n * TOK + (k - 1) * BLK + 1)
                v.tensor_copy(z_bank[k % 2][:, 0:64], bh[:]).then_inc(s["bias_v"], 1)

            def slot(n, t):
                if live(n):
                    rnn_step(n, t)
                if live(n) and t % BLK == BIAS and t // BLK + 1 < TOK // BLK:
                    bias(n, t // BLK + 1)
                if live(n + 1) and t == FIRST_INPUTS - 1:
                    bias(n + 1, 0)
                if live(n):
                    if t == FLUSH[0] + 3:
                        store(n, 0)
                if t == FLUSH[1] + 3 and (not isinstance(n, int) or 1 <= n <= TILES):
                    store(n - 1, 1)
                parts(n, t, att, post)
                if t == TOK - 1:
                    restart()

            walk(dve, slot)

        @block.tensor
        def _(pe):
            t_ = nc.tensor
            pe.wait_ge(s["cond_spread"], 5)
            pe.wait_ge(s["cond_in"], 80)
            pe.wait_ge(s["gconst"], 5)
            for n in range(3):
                for c in range(DC):
                    t_.matmul(bank[n][:, :], cond_rows[:, c, :], wada_sb[:, c, n * 512:(n + 1) * 512],
                              start=(c == 0), stop=False)
                mm = t_.matmul(bank[n][:, :], ones_row[:], bada_row[:, n * 512:(n + 1) * 512], start=False, stop=True)
            mm.then_inc(s["ada_done"], 1)
            pe.wait_ge(s["mod_done"], 5)
            pe.wait_ge(s["w_in"], 16 * 11)

            def turn(dst, src, chunks):
                for c in chunks:
                    mm = t_.transpose(dst[:, c * P:(c + 1) * P], src[:, c * P:(c + 1) * P], ident[:])
                return mm

            def stack_turn(half, bk, stackb=stackb):
                dst = bk[:].bitcast(BF16)
                for h in range(8):
                    mm = t_.transpose(dst[0:96, h * P:(h + 1) * P],
                                      stackb[:, 8 * half + h, :, :].rearrange("p a d -> p (a d)"), ident_bf[:])
                return mm

            def fill(bk, first, last, start):
                n = last - first
                return t_.matmul(bk[:, P * first:P * last].rearrange("p (a n) -> p a n", a=n), ident_bf[:],
                                 ident_bf[:].rearrange("p (a n) -> p a n", a=1).broadcast_to([P, n, P]),
                                 start=start, stop=False, skip_group_check=True)

            def project(m):
                for e in range(2):
                    pe.wait_ge(s["t1_g"], 2 * m + e + 1)
                    wait(pe, s["t1T_a"], 2 * m + e - 1)
                    turn(t_bank[e], t1[:, e, :], range(DC)).then_inc(s["t1_pe"], 1)
                for e in range(2):
                    pe.wait_ge(s["t1T_a"], 2 * m + e + 1)
                    wait(pe, s["y_v"], 2 * m + e - 1)
                    for bk, cols in zip(y_bank[e], (slice(0, 2 * D), slice(2 * D, 3 * D))):
                        for c in range(DC):
                            mm = t_.matmul(bk[:, 0:cols.stop - cols.start], t1T[:, e, c, :], wqkv[:, c, cols],
                                           start=(c == 0), stop=(c == DC - 1))
                    mm.then_inc(s["qkv_pe"], 1)

            def prepare(m, left):
                if left:
                    project(m + 1)
                for e in range(2):
                    pe.wait_ge(s["k3_v"], 2 * m + e + 1)
                    for half, done in enumerate((s["kev_a"], s["kev_v"])):
                        wait(pe, done, 2 * m + e)
                        stack_turn(half, k_bank[half], stack[e]).then_inc(s["kst_pe"], 1)
                for _ in range(PREP_FILL):
                    fill(t_bank[0], 0, 4, True)

            for _ in range(PREP_FILL):
                fill(t_bank[0], 0, 4, True)
            project(0)
            pairs(pe, prepare)

            def att(i, l):
                i1 = i + 1
                if l == QT:
                    pe.wait_ge(s["q3_v"], i1)
                    wait(pe, s["p_a"], 32 * i)
                    stack_turn(0, s_bank[0]).then_inc(s["qst_pe"], 1)
                if l == QT + 1:
                    stack_turn(1, s_bank[1]).then_inc(s["qst_pe"], 1)
                for u in SCORE_UNITS.get(l, ()):
                    g, b, j = u // 8, (u // 4) % 2, u % 4
                    h = QUAD * g + j
                    if u == 0:
                        pe.wait_ge(s["qev_a"], 2 * i1)
                    if u == 1:
                        pe.wait_ge(s["qev_v"], 2 * i1)
                    if u >= 2:
                        pe.wait_ge(s["p_a"], 32 * i + u - 1)
                    for kc in range(KC):
                        mm = t_.matmul(s_bank[u % 2][:, kc * TOK:(kc + 1) * TOK], kT[:, h, b, kc * P:(kc + 1) * P],
                                       qT[:, h, b * TOK:(b + 1) * TOK], start=(kc == 0), stop=(kc == KC - 1),
                                       skip_group_check=True)
                    mm.then_inc(s["s_pe"], 1)
                for k in OUTPUT_CHUNKS.get(l, ()):
                    w, kc = k // KC, k % KC
                    g, b = w // 2, w % 2
                    if kc == 0:
                        pe.wait_ge(s["p_a"], 32 * i + 4 * w + 4)
                        if w == 0:
                            wait(pe, s["o_ev"], i)
                    for j in range(QUAD):
                        mm = t_.matmul(o_bank[32 * j:32 * j + HD + 1, w * TOK:(w + 1) * TOK],
                                       vals[:, kc, b, QUAD * g + j, :], probs[:, w % 2, j, kc * TOK:(kc + 1) * TOK],
                                       start=(kc == 0), stop=(kc == KC - 1), skip_group_check=True)
                    if kc == KC - 1:
                        mm.then_inc(s["pv_pe"], 1)

            def post(i, L):
                i1 = i + 1
                if L == O_TURN:
                    pe.wait_ge(s["o_ev"], i1)
                    wait(pe, s["y1T_a"], 2 * i)
                    turn(a_bank, oT, range(0, 2))
                if L == O_TURN + 1:
                    turn(a_bank, oT, range(2, 4)).then_inc(s["to_pe"], 1)
                if L == Z_TURN:
                    pe.wait_ge(s["zt_v"], i1)
                    turn(a_bank, wc, range(DC)).then_inc(s["z_pe"], 1)
                if WO <= L < WO + DC:
                    c = L - WO
                    if c == 0:
                        pe.wait_ge(s["zc_a"], i1)
                    mm = t_.matmul(b_bank[:, 0:D], aT[:, c, :], wo[:, c, :], start=(c == 0), stop=(c == DC - 1))
                    if c == DC - 1:
                        mm.then_inc(s["wo_pe"], 1)
                if L == T2_TURN:
                    pe.wait_ge(s["t2_v"], i1)
                    turn(a_bank, wb, range(DC)).then_inc(s["t2_pe"], 1)
                if F1 <= L < F1 + FC:
                    n = L - F1
                    if n == 0:
                        pe.wait_ge(s["t2T_a"], i1)
                    bk, o = (a_bank, b_bank)[n // 4], P * (n % 4)
                    for c in range(DC):
                        mm = t_.matmul(bk[:, o:o + P], aT[:, c, :], wf1[:, c, n * P:(n + 1) * P],
                                       start=(c == 0), stop=(c == DC - 1))
                    if n % 4 == 3:
                        mm.then_inc(s["f1_pe"], 1)
                for half, at in enumerate(Y1_TURN):
                    if at <= L < at + 2:
                        c = 2 * (L - at)
                        if c == 0:
                            pe.wait_ge(s["y1_v"], 2 * i + half + 1)
                        mm = turn((a_bank, b_bank)[half], y1[:, 512 * half:512 * half + 512], range(c, c + 2))
                        if c:
                            mm.then_inc(s["y1_pe"], 1)
                if F2 <= L < F2 + FC:
                    c = L - F2
                    if c % 4 == 0:
                        pe.wait_ge(s["y1T_a"], 2 * i + c // 4 + 1)
                    mm = t_.matmul(m_bank[:, 256:512], y1T[:, c, :], wf2[:, c, :], start=(c == 0), stop=(c == FC - 1))
                    if c == FC - 1:
                        mm.then_inc(s["f2_pe"], 1)
                if L == XO_TURN:
                    pe.wait_ge(s["xo_v"], i1)
                    turn(m_bank, xo, range(DC)).then_inc(s["xo_pe"], 1)

            def inputs(k, part):
                z = z_bank[k % 2]
                for j in range(QUAD):
                    dst, cols = z[32 * j:32 * j + ROWS, 0:64], slice(64 * j, 64 * j + 64)
                    t_.matmul(dst, xT[:, part, ROWS * k:ROWS * (k + 1)], wx[:, part, cols], start=False, stop=False,
                              skip_group_check=True)

            def rnn_step(n, t):
                m = t % BLK
                z = z_bank[(t // BLK) % 2]
                base = ROWS * (t if t else TOK) - B * m
                pe.wait_ge(s["h_a"], n * TOK + t + 1)
                for c in range(2):
                    for j in range(QUAD):
                        mm = t_.matmul(z[32 * j:32 * j + ROWS, 0:64], hist[:, c, base:base + ROWS],
                                       wh[:, c, 64 * j:64 * j + 64], start=False, stop=(c == 1 and m == BLK - 1),
                                       skip_group_check=True)
                mm.then_inc(s["z_pe_step"], 1)

            def keep_clock(t, n):
                fill(z_bank[(t // BLK + 1) % 2], 1, 1 + n, False)

            def flush(hh, c):
                for b in range(B):
                    o = ROWS * (HALF * hh + 1)
                    hs = hist[:, c, o:o + ROWS * HALF].rearrange("p (s r) -> p s r", r=ROWS)[:, :, b]
                    q = b * TOK + HALF * hh
                    cols = m_bank[q:q + HALF, 0:D].rearrange("p (j c n) -> p j c n", j=QUAD, c=2)[:, :, c, :]
                    mm = t_.matmul(cols, hs, ident[:].rearrange("p (j n) -> p j n", j=QUAD), start=True, stop=True,
                                   skip_group_check=True)
                if c == 1:
                    mm.then_inc(s["flush_pe"], 1)

            def slot(n, t):
                if live(n):
                    rnn_step(n, t)
                    part = t % BLK - INPUTS
                    if 0 <= part < DC and t // BLK + 1 < TOK // BLK:
                        if part == 0:
                            pe.wait_ge(s["bias_v"], TOK // BLK * n + t // BLK + 2)
                        inputs(t // BLK + 1, part)
                    if t in (FLUSH[0], FLUSH[0] + 1):
                        if t == FLUSH[0]:
                            pe.wait_ge(s["xT_a"], n + 1)
                        flush(0, t - FLUSH[0])
                if t in (FLUSH[1], FLUSH[1] + 1) and (not isinstance(n, int) or 1 <= n <= TILES):
                    if t == FLUSH[1]:
                        if not live(n):
                            pe.wait_ge(s["h_a"], TILES * TOK + 1)
                            pe.wait_ge(s["xT_a"], TILES)
                        else:
                            pe.wait_ge(s["xT_a"], n + 1)
                        pe.wait_ge(s["out_v"], 2 * n - 1)
                    flush(1, t - FLUSH[1])
                if live(n) and t % BLK != BIAS and t not in (FIRST_INPUTS - 1, FIRST_INPUTS):
                    for width in spare(n, t):
                        keep_clock(t, width)
                if isinstance(n, int) and n in (-2, -1) and FIXED[(t + LEAD) % TOK] < 2:
                    fill(z_bank[1], 1, 3, False)
                parts(n, t, att, post)
                if live(n + 1) and FIRST_INPUTS <= t < FIRST_INPUTS + DC:
                    if t == FIRST_INPUTS:
                        pe.wait_ge(s["xT_a"], n + 2)
                        pe.wait_ge(s["bias_v"], TOK // BLK * (n + 1) + 1)
                    inputs(0, t - FIRST_INPUTS)

            pe.wait_ge(s["kev_a"], TILES)
            pe.wait_ge(s["kev_v"], TILES)
            pe.wait_ge(s["y_v"], TILES)
            pe.wait_ge(s["v_g"], TILES)
            pe.wait_ge(s["o_mem"], 1)
            for z in z_bank:
                fill(z, 0, 4, True).then_inc(s["bits_pe"], 1)
            walk(pe, slot)


_INS = ['x', 'cond_1024', 'L0_cond_w_q', 'L0_cond_b_q', 'L0_cond_w_k', 'L0_cond_b_k', 'L0_cond_w_v', 'L0_cond_b_v',
        'L0_cond_w_o', 'L0_cond_b_o', 'L0_cond_w_f1', 'L0_cond_b_f1', 'L0_cond_w_f2', 'L0_cond_b_f2',
        'L0_cond_w_ada', 'L0_cond_b_ada', 'L1_cond_Wx', 'L1_cond_Wh', 'L1_cond_b']


def kernel(**inputs):
    import numpy as _np
    import concourse.bacc as _bacc
    from concourse import mybir as _mybir
    from concourse.bass_utils import run_bass_kernel_spmd as _run

    nc = _bacc.Bacc("TRN2", target_bir_lowering=False, num_devices=1)
    arrays, args = {}, []
    for name in _INS:
        a = _np.ascontiguousarray(inputs[name])
        arrays[f"in_{name}_dram"] = a
        args.append(nc.dram_tensor(f"in_{name}_dram", a.shape, _mybir.dt.from_np(a.dtype), kind="ExternalInput").ap())
    args.append(nc.dram_tensor("out_0_dram", (2, 1024, 256), _mybir.dt.float32, kind="ExternalOutput").ap())
    build(nc, *args)
    r = _run(nc, [arrays], core_ids=[0])
    return r.results[0]["out_0_dram"]
```
